# Optimizing a Trainium2 kernel written in Bass

```python
import numpy as np
import jax
import jax.numpy as jnp

def _softmax(x, axis=-1):
    return jax.nn.softmax(x, axis=axis)

def _gelu(x):
    return jax.nn.gelu(x, approximate=True)

def _silu(x):
    return jax.nn.silu(x)

def _sigmoid(x):
    return jax.nn.sigmoid(x)

def _layernorm(x, axis=-1, eps=1e-05):
    m = jnp.mean(x, axis=axis, keepdims=True)
    v = jnp.var(x, axis=axis, keepdims=True)
    return (x - m) / jnp.sqrt(v + eps)

def _scatter_add(tgt, idx, src, axis=0):
    return tgt.at[idx].add(src)

def _segment_sum(src, seg, n):
    return jax.ops.segment_sum(src, seg, n)
kernel_name = 'mk_flamingo_gated_d1_seqx_r8_48cafe'

def setup_inputs(seed: int=0):
    np.random.seed(seed)
    _w = jnp.asarray

    def _rec_inputs():
        import jax
        import jax.numpy as jnp
        _rk = jax.random.key(seed)
        x = -0.0003929 + 0.9999 * jax.random.normal(jax.random.fold_in(_rk, 1), (16, 128, 128), jnp.float32)
        _lenS = 128 - jax.random.randint(jax.random.fold_in(_rk, 7), (16,), 0, max(1, 128 // 4) + 1, jnp.int32)
        _lenS2 = 77 - jax.random.randint(jax.random.fold_in(_rk, 8), (16,), 0, max(1, 77 // 4) + 1, jnp.int32)
        _ctx_1024P = jax.random.normal(jax.random.fold_in(_rk, 11), (16, 16, 128), jnp.float32)
        _ctx_1024c = jax.random.dirichlet(jax.random.fold_in(_rk, 511), 0.3 * jnp.ones((16,), jnp.float32), (16, 77))
        _ctx_1024t = jnp.einsum('bsk,bkd->bsd', _ctx_1024c, _ctx_1024P)
        _ctx_1024t = _ctx_1024t * jax.lax.rsqrt(jnp.mean(jnp.square(_ctx_1024t)) + 1e-12) * 0.953939
        ctx_1024 = 4.13588e-05 + 0.999923 * (_ctx_1024t + 0.3 * jax.random.normal(jax.random.fold_in(_rk, 611), (16, 77, 128), jnp.float32))
        _g = jax.random.normal(jax.random.fold_in(_rk, 9001), (2, 1), jnp.float32)
        _g = jnp.sign(_g) * jnp.maximum(jnp.abs(_g), 1.0) + (_g == 0) * 1.0
        g_xattn = _g[0]
        g_ffn = _g[1]
        return (x, ctx_1024, g_xattn, g_ffn)
    x, ctx_1024, g_xattn, g_ffn = _rec_inputs()

    def _L0_xattn_setup():
        import jax, jax.numpy as jnp
        import numpy as np
        H = 128
        B = 8
        L_CHAR = 256
        L_SUB = 128

        def _linear(x, W, b):
            return jnp.einsum('blh,oh->blo', x, W) + b

        def _interp_linear(x, out_len):
            L_in = x.shape[1]
            pos = (jnp.arange(out_len, dtype=x.dtype) + 0.5) * (L_in / out_len) - 0.5
            pos = jnp.clip(pos, 0.0, L_in - 1)
            lo = jnp.floor(pos).astype(jnp.int32)
            hi = jnp.minimum(lo + 1, L_in - 1)
            w = (pos - lo.astype(x.dtype))[None, :, None]
            return x[:, lo] * (1 - w) + x[:, hi] * w
        key = jax.random.key(seed)
        ks = jax.random.split(key, 18)
        s = 0.02
        inp = {'char_emb': jax.random.normal(ks[0], (B, L_CHAR, H), jnp.float32), 'subword_emb': jax.random.normal(ks[1], (B, L_SUB, H), jnp.float32)}
        names = ['Wq_c', 'Wk_s', 'Wv_s', 'Wq_s', 'Wk_c', 'Wv_c']
        for i, n in enumerate(names):
            inp[n] = jax.random.normal(ks[2 + 2 * i], (H, H), jnp.float32) * s
            inp['b' + n[1:]] = jax.random.normal(ks[3 + 2 * i], (H,), jnp.float32) * s
        inp['Wg'] = jax.random.normal(ks[14], (H, 2 * H), jnp.float32) * s
        inp['bg'] = jax.random.normal(ks[15], (H,), jnp.float32) * s
        return inp
    _L0_xattn_all = _L0_xattn_setup()
    _L0_xattn_in = {k: v for k, v in _L0_xattn_all.items() if k in ('Wq_c', 'bq_c', 'Wk_s', 'bk_s', 'Wv_s', 'bv_s', 'Wq_s', 'bq_s', 'Wk_c', 'bk_c', 'Wv_c', 'bv_c', 'Wg', 'bg')}
    del _L0_xattn_all

    def _L0_ffn_setup():
        import jax, jax.numpy as jnp
        import numpy as np
        E, TOP_K, D, H = (8, 2, 128, 256)
        B, S = (2, 256)
        key = jax.random.key(seed)
        ks = jax.random.split(key, 10)
        s = 0.02
        return {'x': jax.random.normal(ks[0], (B, S, D), dtype=jnp.float32), 'gate_w': jax.random.normal(ks[1], (E, D), dtype=jnp.float32) * s, 'gate_b': jnp.zeros((E,), dtype=jnp.float32), 'w0': jax.random.normal(ks[2], (E, H, D), dtype=jnp.float32) * s, 'b0': jnp.zeros((E, H), dtype=jnp.float32), 'w1': jax.random.normal(ks[3], (E, H, D), dtype=jnp.float32) * s, 'b1': jnp.zeros((E, H), dtype=jnp.float32), 'w2': jax.random.normal(ks[4], (E, D, H), dtype=jnp.float32) * s, 'b2': jnp.zeros((E, D), dtype=jnp.float32)}
    _L0_ffn_all = _L0_ffn_setup()
    _L0_ffn_in = {k: v for k, v in _L0_ffn_all.items() if k in ('gate_w', 'gate_b', 'w0', 'b0', 'w1', 'b1', 'w2', 'b2')}
    del _L0_ffn_all
    return {'x': x, 'ctx_1024': ctx_1024, 'g_xattn': g_xattn, 'g_ffn': g_ffn, 'L0_xattn_Wq_c': _L0_xattn_in['Wq_c'], 'L0_xattn_bq_c': _L0_xattn_in['bq_c'], 'L0_xattn_Wk_s': _L0_xattn_in['Wk_s'], 'L0_xattn_bk_s': _L0_xattn_in['bk_s'], 'L0_xattn_Wv_s': _L0_xattn_in['Wv_s'], 'L0_xattn_bv_s': _L0_xattn_in['bv_s'], 'L0_xattn_Wq_s': _L0_xattn_in['Wq_s'], 'L0_xattn_bq_s': _L0_xattn_in['bq_s'], 'L0_xattn_Wk_c': _L0_xattn_in['Wk_c'], 'L0_xattn_bk_c': _L0_xattn_in['bk_c'], 'L0_xattn_Wv_c': _L0_xattn_in['Wv_c'], 'L0_xattn_bv_c': _L0_xattn_in['bv_c'], 'L0_xattn_Wg': _L0_xattn_in['Wg'], 'L0_xattn_bg': _L0_xattn_in['bg'], 'L0_ffn_gate_w': _L0_ffn_in['gate_w'], 'L0_ffn_gate_b': _L0_ffn_in['gate_b'], 'L0_ffn_w0': _L0_ffn_in['w0'], 'L0_ffn_b0': _L0_ffn_in['b0'], 'L0_ffn_w1': _L0_ffn_in['w1'], 'L0_ffn_b1': _L0_ffn_in['b1'], 'L0_ffn_w2': _L0_ffn_in['w2'], 'L0_ffn_b2': _L0_ffn_in['b2']}

def reference(x, ctx_1024, g_xattn, g_ffn, L0_xattn_Wq_c, L0_xattn_bq_c, L0_xattn_Wk_s, L0_xattn_bk_s, L0_xattn_Wv_s, L0_xattn_bv_s, L0_xattn_Wq_s, L0_xattn_bq_s, L0_xattn_Wk_c, L0_xattn_bk_c, L0_xattn_Wv_c, L0_xattn_bv_c, L0_xattn_Wg, L0_xattn_bg, L0_ffn_gate_w, L0_ffn_gate_b, L0_ffn_w0, L0_ffn_b0, L0_ffn_w1, L0_ffn_b1, L0_ffn_w2, L0_ffn_b2):
    import jax
    import jax.numpy as jnp

    def _L0_xattn_ref(char_emb, subword_emb, Wq_c, bq_c, Wk_s, bk_s, Wv_s, bv_s, Wq_s, bq_s, Wk_c, bk_c, Wv_c, bv_c, Wg, bg):
        import jax, jax.numpy as jnp
        import numpy as np
        H = 128
        B = 8
        L_CHAR = 256
        L_SUB = 128

        def _linear(x, W, b):
            return jnp.einsum('blh,oh->blo', x, W) + b

        def _interp_linear(x, out_len):
            L_in = x.shape[1]
            pos = (jnp.arange(out_len, dtype=x.dtype) + 0.5) * (L_in / out_len) - 0.5
            pos = jnp.clip(pos, 0.0, L_in - 1)
            lo = jnp.floor(pos).astype(jnp.int32)
            hi = jnp.minimum(lo + 1, L_in - 1)
            w = (pos - lo.astype(x.dtype))[None, :, None]
            return x[:, lo] * (1 - w) + x[:, hi] * w
        h = char_emb.shape[-1]
        scale = 1.0 / jnp.sqrt(jnp.asarray(h, char_emb.dtype))
        Q_char = _linear(char_emb, Wq_c, bq_c)
        K_sub = _linear(subword_emb, Wk_s, bk_s)
        V_sub = _linear(subword_emb, Wv_s, bv_s)
        scores = jnp.einsum('bqh,bkh->bqk', Q_char, K_sub) * scale
        char2sub = jnp.einsum('bqk,bkh->bqh', jax.nn.softmax(scores, axis=-1), V_sub)
        Q_sub = _linear(subword_emb, Wq_s, bq_s)
        K_char = _linear(char_emb, Wk_c, bk_c)
        V_char = _linear(char_emb, Wv_c, bv_c)
        scores2 = jnp.einsum('bqh,bkh->bqk', Q_sub, K_char) * scale
        sub2char = jnp.einsum('bqk,bkh->bqh', jax.nn.softmax(scores2, axis=-1), V_char)
        L_char = char_emb.shape[1]
        if sub2char.shape[1] != L_char:
            sub2char = _interp_linear(sub2char, L_char)
        gate_in = jnp.concatenate([char2sub, sub2char], axis=-1)
        gate = jax.nn.sigmoid(jnp.einsum('blh,oh->blo', gate_in, Wg) + bg)
        return gate * char2sub + (1 - gate) * sub2char

    def _L0_ffn_ref(x, gate_w, gate_b, w0, b0, w1, b1, w2, b2):
        import jax, jax.numpy as jnp
        import numpy as np
        E, TOP_K, D, H = (8, 2, 128, 256)
        B, S = (2, 256)
        Bn, Sq, Dv = x.shape
        xt = x.reshape(-1, Dv)
        logits = xt @ gate_w.T + gate_b
        top_v, top_i = jax.lax.top_k(logits, TOP_K)
        h0 = jnp.einsum('td,ehd->eth', xt, w0) + b0[:, None, :]
        h1 = jnp.einsum('td,ehd->eth', xt, w1) + b1[:, None, :]
        act = h0 * jax.nn.silu(h1)
        out_all = jnp.einsum('eth,edh->etd', act, w2) + b2[:, None, :]
        out_te = jnp.transpose(out_all, (1, 0, 2))
        sel = jnp.take_along_axis(out_te, top_i[:, :, None], axis=1)
        w = jax.nn.softmax(top_v, axis=-1)[:, :, None]
        out = (w * sel).sum(axis=1)
        return out.reshape(Bn, Sq, Dv)
    x = x + jnp.tanh(g_xattn[0]) * _L0_xattn_ref(_layernorm(x, axis=-1), ctx_1024, L0_xattn_Wq_c, L0_xattn_bq_c, L0_xattn_Wk_s, L0_xattn_bk_s, L0_xattn_Wv_s, L0_xattn_bv_s, L0_xattn_Wq_s, L0_xattn_bq_s, L0_xattn_Wk_c, L0_xattn_bk_c, L0_xattn_Wv_c, L0_xattn_bv_c, L0_xattn_Wg, L0_xattn_bg)
    x = x + jnp.tanh(g_ffn[0]) * _L0_ffn_ref(_layernorm(x, axis=-1), L0_ffn_gate_w, L0_ffn_gate_b, L0_ffn_w0, L0_ffn_b0, L0_ffn_w1, L0_ffn_b1, L0_ffn_w2, L0_ffn_b2)
    return x

_drawn_inputs = setup_inputs


def setup_inputs(seed=0):
    import zlib

    import numpy as np

    out = dict(_drawn_inputs(seed))
    spreads = {'L0_ffn_gate_b': (0.0, 0.1),
     'L0_ffn_b0': (0.0, 0.8),
     'L0_ffn_b1': (0.0, 0.8),
     'L0_ffn_b2': (0.0, 0.58)}
    factors = {'L0_xattn_Wq_c': 8.0,
     'L0_xattn_bq_c': 8.0,
     'L0_xattn_Wk_s': 8.0,
     'L0_xattn_bk_s': 64.0,
     'L0_xattn_bv_s': 6.037,
     'L0_xattn_Wq_s': 8.0,
     'L0_xattn_bq_s': 8.0,
     'L0_xattn_Wk_c': 8.0,
     'L0_xattn_bk_c': 64.0,
     'L0_xattn_Wv_c': 6.104,
     'L0_xattn_bv_c': 6.028,
     'L0_xattn_Wg': 8.0,
     'L0_xattn_bg': 8.0,
     'L0_ffn_w0': 8.0,
     'L0_ffn_w1': 8.0,
     'L0_ffn_w2': 8.0}
    for name, (base, spread) in spreads.items():
        noise = np.random.default_rng([zlib.crc32(name.encode()), seed]).standard_normal(out[name].shape)
        drawn = base * np.exp(spread * noise) if base else spread * noise
        out[name] = jnp.asarray(drawn.astype(out[name].dtype))
    for name, factor in factors.items():
        out[name] = (out[name] * factor).astype(out[name].dtype)
    return out
```

```python
from contextlib import ExitStack

import concourse.bass as bass
from concourse import mybir

F32 = mybir.dt.float32
F32R = mybir.dt.float32r
BF16 = mybir.dt.bfloat16
I32 = mybir.dt.int32
ALU = mybir.AluOpType
ACT = mybir.ActivationFunctionType
AX = mybir.AxisListType.X

B = 16
L = 128
D = 128
S = 77
E = 8
H = 256
G = 2
NG = B // G
NQ = NG // 2
T = B * L
SCALE = 1.0 / float(D) ** 0.5
EPS = 1e-5
FAR = 1.0e30

LIST = T + L
NBLK = 2 * T // L + E - 1
IDLE = E - 1
ROW = D + 4
XS_ROWS = E * LIST + IDLE * L
Y_ROWS = 2 * T + (E + IDLE) * L

W_NAMES = ["Wq_c", "Wk_s", "Wq_s", "Wk_c", "Wv_s", "Wv_c", "WvT_s", "WvT_c", "WgT_1", "WgT_2"]
V_NAMES = ["bq_c", "bk_s", "bq_s", "bk_c", "bv_s", "bv_c", "bg", "g_x", "g_f"]
N_PACK = len(W_NAMES) * D + len(V_NAMES) + 2 * E
C_ID, C_IT, C_LT, C_UT, C_REV, C_BASE, C_JS, C_LIST = 0, 128, 256, 384, 392, 400, 408, 408 + NBLK
N_CONST = C_LIST + E


def flamingo_kernel(nc, x, ctx_in, wpack, w01, w2, b0, b1, b2, consts, dests, pads, out):
    xs = nc.dram_tensor("xs_lists", (XS_ROWS, ROW), F32).ap()
    ys = nc.dram_tensor("y_rows", (Y_ROWS, D), F32).ap()
    stack = ExitStack()
    with stack:
        def sb(name, shape, dt=F32):
            return stack.enter_context(nc.sbuf_tensor(name, shape, dt))

        def sem(name):
            return stack.enter_context(nc.semaphore(name))

        x_res = sb("x_res", [128, B, D])
        c_in = sb("c_in", [S, 2, G, D])
        pack = sb("pack", [128, N_PACK])
        cst = sb("cst", [128, N_CONST])
        dest = sb("dest", [128, 2, B], I32)
        pad = sb("pad", [128, E + IDLE, ROW])
        W = {n: pack[:, i * D:(i + 1) * D] for i, n in enumerate(W_NAMES)}
        V = {n: pack[:, len(W_NAMES) * D + i:len(W_NAMES) * D + i + 1] for i, n in enumerate(V_NAMES)}
        o = len(W_NAMES) * D + len(V_NAMES)
        gate_wT, gate_bB = pack[:, o:o + E], pack[:, o + E:o + 2 * E]
        ident = cst[:, C_ID:C_ID + 128]
        interpT = cst[0:S, C_IT:C_IT + L]

        A1T = sb("A1T", [128, D])
        A2T = sb("A2T", [128, D])
        U1 = sb("U1", [128, D])
        AG1T = sb("AG1T", [128, D])
        AG2T = sb("AG2T", [128, D])
        bq_rep = sb("bq_rep", [128, 2, D])
        vec = sb("vec", [128, 8])
        g1b, g2b, u2, k1s, k2s, bth, tgx, tgf = (vec[:, i:i + 1] for i in range(8))
        lt16 = sb("lt16", [128, 128], BF16)
        one16 = sb("one16", [128, 128], BF16)
        ones = sb("ones", [128, 8])

        stat = sb("stat", [128, 2, 2, G, 6])
        mv = sb("mv", [128, 2, 2, G, 2])
        var = sb("var", [128, 2, 2, G])
        rstd = sb("rstd", [128, 2, 2, G])
        halfn = sb("halfn", [128, G])
        xln = sb("xln", [128, 2, G, D])
        tT = sb("tT", [128, 2, G * L + G * S])
        Gs = sb("Gs", [128, 2, 2, G * S])
        sr = sb("sr", [128, 2, 2 * G])
        mx = sb("mx", [128, 2, 2 * G])
        tot = sb("tot", [128, 2, 2 * G])
        nb = sb("nb", [128, 2, 2 * G])
        rs = sb("rs", [128, 2, 2 * G])
        rcp = sb("rcp", [128, 2, 2 * G])
        P1 = sb("P1", [128, 2, G, 128])
        P2 = sb("P2", [S, 2, G, 128])
        PT = sb("PT", [128, 2, 2, G, 128])
        TT = sb("TT", [128, 2, 2, G * L])
        s2c = sb("s2c", [128, 2, G * L])
        th = sb("th", [128, 2, G * L])
        dif = sb("dif", [128, 2, G * L])
        gd = sb("gd", [128, 2, G * L])
        mix = sb("mix", [128, 2, G * L])
        rows = sb("rows", [128, B, 2, ROW])
        x3T = sb("x3T", [128, 2, G * L])

        Q = 2 * G
        lg = sb("lg", [128, Q, E])
        lg2 = sb("lg2", [128, Q, E])
        m1 = sb("m1", [128, B])
        m2 = sb("m2", [128, B])
        eq = sb("eq", [128, Q, E])
        key = sb("key", [128, Q, E])
        km = sb("km", [128, Q])
        oh = sb("oh", [128, 2, Q, E])
        ohs = sb("ohs", [128, Q, E], BF16)
        ohq = sb("ohq", [128, E])
        acc = sb("acc", [128, NQ + 1, E], BF16)
        rk = sb("rk", [128, Q, E])
        prod = sb("prod", [128, 2, Q, E])
        pos = sb("pos", [128, NQ, 2, Q], I32)

        nrow = sb("nrow", [1, E])
        nrow_i = sb("nrow_i", [1, E], I32)
        nbk_i = sb("nbk_i", [E, 1], I32)
        nbk = sb("nbk", [E, 1])
        bcum = sb("bcum", [E, 1])
        cmp = sb("cmp", [E, NBLK])
        es = sb("es", [1, 2, NBLK])
        e_i = sb("e_i", [1, NBLK], I32)
        off = sb("off", [1, NBLK])
        r_i = sb("r_i", [1, NBLK], I32)
        wd = sb("wd", [128, 4, B])

        w01_f = sb("w01_f", [128, E, 2 * H])
        w01_h = sb("w01_h", [128, E, 2 * H], F32R)
        w01_l = sb("w01_l", [128, E, 2 * H], F32R)
        w2_f = sb("w2_f", [128, E, 2, D])
        b0_B = sb("b0_B", [128, E, H])
        b2_B = sb("b2_B", [128, E, D])
        b1_p = sb("b1_p", [128, E * H])
        b1_r = sb("b1_r", [128, E * H])
        b1_s = sb("b1_s", [128, E, H], BF16)
        sel3 = sb("sel3", [128, 128], BF16)
        NX = 4
        xb = sb("xb", [128, NX, ROW])
        xh = sb("xh", [128, 2, 128], F32R)
        xl = sb("xl", [128, 2, 128], F32R)
        sl = sb("sl", [128, 2, H])
        hb = sb("hb", [128, 2, H])
        ab = sb("ab", [128, 2, H])
        aT = sb("aT", [128, 2, H])
        yb = sb("yb", [128, NX, D])
        yin = sb("yin", [128, NQ, 2, Q, D])
        o1 = sb("o1", [128, NQ, Q, D])

        bank = [stack.enter_context(nc.psum_tensor(f"bank{i}", [128, 512], F32)) for i in range(8)]

        s_pack, s_cst, s_dest, s_pad, s_w01, s_w2, s_b0, s_b1, s_b2 = (
            sem("in_" + n) for n in "pack cst dest pad w01 w2 b0 b1 b2".split())
        s_x = [sem(f"in_x{q}") for q in range(NQ)]
        s_c = [sem(f"in_c{p}") for p in range(2)]
        s_setup = sem("setup_memsets")
        s_fold = sem("fold_products")
        s_folded = sem("folded_weights")
        s_var1, s_rstd1, s_xln = sem("var1"), sem("rstd1"), sem("xln")
        s_tp, s_tT, s_g, s_gs, s_sc = sem("xc_transposed"), sem("xc_T_in_sbuf"), sem("G_made"), sem("G_in_sbuf"), sem("scores")
        s_nb, s_exp, s_prob = sem("neg_max"), sem("exps"), sem("probs")
        s_pt, s_ptc, s_t, s_tt = sem("probs_T"), sem("probs_T_in_sbuf"), sem("t_products"), sem("t_in_sbuf")
        s_mixp, s_gate, s_mix, s_mT, s_x2 = sem("mix_products"), sem("gate_tanh"), sem("mix"), sem("mix_T"), sem("x2")
        s_var2, s_rstd2, s_rows = sem("var2"), sem("rstd2"), sem("rows_ready")
        s_x3p, s_x3T, s_lg = sem("x3_transposed"), sem("x3T_in_sbuf"), sem("logits")
        s_lgr = sem("logits_read")
        s_oh, s_rank, s_rkr, s_pos = sem("one_hots"), sem("ranks"), sem("ranks_read"), sem("positions")
        s_scat = sem("scattered")
        s_cnt, s_nrow, s_padw = sem("counts"), sem("counts_in_sbuf"), sem("pads_written")
        s_tab = sem("table_products")
        s_tabv = sem("table_steps")
        s_table = sem("tables_ready")
        s_wsp = sem("w01_hi")
        s_wsl = sem("w01_lo")
        s_b1s = sem("b1_split")
        s_xb = [sem(f"block_in{b}") for b in range(NX)]
        s_sc2 = [sem(f"block_out{b}") for b in range(NX)]
        s_f1, s_f2, s_f3, s_f4, s_f5, s_f6 = (sem(n) for n in "blk_xT blk_hi blk_lo blk_h blk_silu blk_act".split())
        s_f6a = sem("blk_h0")
        s_f7, s_f8, s_f9, s_f10 = (sem(n) for n in "blk_aT blk_aT_in_sbuf blk_y blk_y_in_sbuf".split())
        s_seen = sem("block_seen")
        s_yin = [sem(f"y_in{q}") for q in range(NQ)]
        s_o1 = sem("first_choice_added")
        s_fin = sem("final_rows")
        s_out = sem("stored")
        s_wts = sem("choice_weights")
        s_v = sem("vector_step")
        s_a = sem("scalar_step")

        block = stack.enter_context(nc.Block())

        xv = x.rearrange("b l d -> l b d")
        cv = ctx_in.rearrange("b l d -> l b d")
        ov = out.rearrange("b l d -> l b d")
        yv = ys[0:2 * T, :].rearrange("(k b l) d -> l k b d", k=2, b=B)

        @block.sync
        def _(sp):
            def load_c(g):
                if g >= 2:
                    sp.wait_ge(s_t, g - 1)
                sp.dma_start(c_in[:, g % 2, :, :], cv[:, G * g:G * g + G, :]).then_inc(s_c[g % 2], 16)

            sp.dma_start(x_res[:, 0:Q, :], xv[:, 0:Q, :]).then_inc(s_x[0], 16)
            sp.dma_start(pack[:, :], wpack).then_inc(s_pack, 16)
            load_c(0)
            load_c(1)
            for q in range(1, NQ):
                sp.dma_start(x_res[:, q * Q:q * Q + Q, :], xv[:, q * Q:q * Q + Q, :]).then_inc(s_x[q], 16)
            sp.dma_start(b1_p[:, :], b1).then_inc(s_b1, 16)
            sp.dma_start(dest[:, :, :], dests).then_inc(s_dest, 16)
            for g in range(2, NG):
                load_c(g)
            sp.dma_start(xs[E * LIST:XS_ROWS, :].rearrange("(i p) d -> p i d", p=L),
                         pad[:, E:E + IDLE, :]).then_inc(s_padw, 16)
            sp.wait_ge(s_nrow, 1)
            for e in range(E):
                n = sp.value_load(nrow_i[0:1, e:e + 1], min_val=0, max_val=T)
                sp.dma_start(xs[bass.ds(n + e * LIST, L), :], pad[:, e, :]).then_inc(s_padw, 16)
            sp.wait_ge(s_table, 1)
            sp.wait_ge(s_padw, 16 * (E + 1))
            sp.wait_ge(s_scat, 16 * 2 * B)

            def load_block(j, b):
                r = sp.value_load(r_i[0:1, bass.ds(j, 1)], min_val=0, max_val=XS_ROWS - L)
                sp.dma_start(xb[:, b, :], xs[bass.ds(r, L), :]).then_inc(s_xb[b], 16)

            for j in range(NX):
                load_block(j, j)
            with sp.Fori(0, NBLK // NX - 1) as i:
                for b in range(NX):
                    sp.wait_ge(s_sc2[b], 16 * (i + 1))
                    load_block(i * NX + (b + NX), b)
            for j in range(NBLK // NX * NX, NBLK):
                sp.wait_ge(s_sc2[j % NX], 16 * (j // NX))
                load_block(j, j % NX)
            for b in range(NX):
                sp.wait_ge(s_sc2[b], 16 * len(range(b, NBLK, NX)))
            for q in range(NQ):
                for k in range(2):
                    sp.dma_start(yin[:, q, k, :, :], yv[:, k, q * Q:q * Q + Q, :]).then_inc(s_yin[q], 16)
            for q in range(NQ):
                sp.wait_ge(s_fin, q + 1)
                sp.dma_start(ov[:, q * Q:q * Q + Q, :], x_res[:, q * Q:q * Q + Q, :]).then_inc(s_out, 16)
            sp.wait_ge(s_out, 16 * NQ)

        @block.gpsimd
        def _(pool):
            pool.memset(halfn[:, :], -0.5).then_inc(s_setup, 1)
            pool.memset(one16[:, :], 1.0).then_inc(s_setup, 1)
            pool.memset(ones[:, :], 1.0).then_inc(s_setup, 1)
            pool.memset(P1[:, :, :, S:128], 0.0).then_inc(s_setup, 1)
            pool.memset(acc[:, 0, :], 0.0).then_inc(s_setup, 1)
            pool.memset(sr[:, :, :], 0.0).then_inc(s_setup, 1)
            pool.memset(mx[:, :, :], 0.0).then_inc(s_setup, 1)
            pool.memset(rs[:, :, :], 1.0).then_inc(s_setup, 1)
            pool.memset(sel3[:, :], 1.0).then_inc(s_setup, 1)
            pool.wait_ge(s_setup, 9)

            def power(n, g, have, done):
                pool.wait_ge(have, g + 1)
                pool.tensor_tensor(rstd[:, n, g % 2, :], var[:, n, g % 2, :], halfn[:, :],
                                   ALU.pow).then_inc(done, 1)

            power(0, 0, s_var1, s_rstd1)
            for i in range(NG + 3):
                g = i - 3
                if g >= 0:
                    power(1, g, s_var2, s_rstd2)
                if i + 1 < NG:
                    power(0, i + 1, s_var1, s_rstd1)
                if g >= 0:
                    if g % 2:
                        q = g // 2
                        pool.wait_ge(s_pos, q + 1)
                        pool.wait_ge(s_rows, g + 1)
                        for j in range(Q):
                            for k in range(2):
                                pool.indirect_dma_start(
                                    xs, bass.IndirectOffsetOnAxis(ap=pos[:, q, k, j:j + 1], axis=0),
                                    rows[:, q * Q + j, k, :], None).then_inc(s_scat, 16)

            def scatter(j, b):
                pool.wait_ge(s_f10, j + 1)
                pool.sem_inc(s_seen, 1)
                pool.indirect_dma_start(
                    ys, bass.IndirectOffsetOnAxis(ap=xb[:, b, D:D + 1].bitcast(I32), axis=0),
                    yb[:, b, :], None).then_inc(s_sc2[b], 16)

            with pool.Fori(0, NBLK // NX) as i:
                for b in range(NX):
                    scatter(i * NX + b, b)
            for j in range(NBLK // NX * NX, NBLK):
                scatter(j, j % NX)

        @block.scalar
        def _(act):
            act.dma_start(cst[:, :], consts).then_inc(s_cst, 16)
            act.dma_start(pad[:, :, :], pads).then_inc(s_pad, 16)
            act.dma_start(w01_f[:, :, :], w01).then_inc(s_w01, 16)
            act.dma_start(w2_f[:, :, :, :], w2).then_inc(s_w2, 16)
            act.dma_start(b0_B[:, :, :], b0.partition_broadcast(128)).then_inc(s_b0, 16)
            act.dma_start(b2_B[:, :, :], b2.partition_broadcast(128)).then_inc(s_b2, 16)
            act.wait_ge(s_cst, 16)
            act.activation(lt16[:, :], cst[:, C_LT:C_LT + 128], ACT.Copy).then_inc(s_folded, 1)
            act.wait_ge(s_pack, 16)
            act.activation(tgx, V["g_x"], ACT.Tanh).then_inc(s_folded, 1)
            act.activation(tgf, V["g_f"], ACT.Tanh).then_inc(s_folded, 1)
            act.wait_ge(s_fold, 1)
            for i, dst in enumerate((A1T, A2T, U1)):
                act.activation(dst[:, :], bank[0][:, i * D:i * D + D], ACT.Copy).then_inc(s_folded, 1)
            act.wait_ge(s_fold, 2)
            for i, dst in enumerate((AG1T, AG2T)):
                act.activation(dst[:, :], bank[1][:, i * D:i * D + D], ACT.Copy).then_inc(s_folded, 1)
            act.wait_ge(s_fold, 3)
            for i, (dst, sc) in enumerate(((g1b, 1.0), (g2b, 1.0), (u2, 1.0), (k1s, SCALE), (k2s, SCALE), (bth, 0.5))):
                ins = act.activation(dst, bank[2][:, i:i + 1], ACT.Copy, scale=sc)
                ins.then_inc(s_folded, 1)
            act.wait_ge(s_folded, 14)
            act.wait_ge(s_setup, 9)
            for p in range(2):
                for j in range(G):
                    act.activation(sr[:, p, j:j + 1], k1s, ACT.Copy).then_inc(s_folded, 1)

            def A2(g):
                act.wait_ge(s_tp, g + 1)
                if g >= 2:
                    act.wait_ge(s_sc, g - 1)
                act.activation(tT[:, g % 2, :], bank[0][:, 0:G * L + G * S], ACT.Copy).then_inc(s_tT, 1)

            def A4(g):
                p = g % 2
                act.wait_ge(s_g, g + 1)
                if g >= 2:
                    act.wait_ge(s_sc, g - 1)
                    act.wait_ge(s_nb, g - 1)
                act.activation(Gs[:, p, 0, :], bank[1][:, 0:G * S], ACT.Identity, bias=g1b).then_inc(s_gs, 1)
                act.activation(Gs[:, p, 1, :], bank[1][:, G * S:2 * G * S], ACT.Identity, bias=g2b).then_inc(s_gs, 1)
                act.activation(sr[0:S, p, G:2 * G], bank[1][0:S, 2 * G * S:2 * G * S + G], ACT.Identity,
                               bias=k2s[0:S, :], scale=SCALE).then_inc(s_gs, 1)

            def B2(g):
                p = g % 2
                act.wait_ge(s_nb, g + 1)
                if g >= 2:
                    act.wait_ge(s_pt, g - 1)
                for j in range(G):
                    act.activation(P1[:, p, j, 0:S], bank[2][:, j * S:j * S + S], ACT.Exp, bias=nb[:, p, j:j + 1],
                                   scale=SCALE, accum_out=rs[:, p, j:j + 1])
                for j in range(G):
                    ins = act.activation(P2[:, p, j, :], bank[2][0:S, 256 + j * L:256 + j * L + L], ACT.Exp,
                                         bias=nb[0:S, p, G + j:G + j + 1], scale=SCALE,
                                         accum_out=rs[0:S, p, G + j:G + j + 1])
                ins.then_inc(s_exp, 1)

            def B5(g):
                act.wait_ge(s_pt, g + 1)
                if g >= 2:
                    act.wait_ge(s_t, g - 1)
                act.activation(PT[:, g % 2, :, :, :].rearrange("p a b c -> p (a b c)"), bank[3][:, :],
                               ACT.Copy).then_inc(s_ptc, 1)

            def C2(g):
                p = g % 2
                act.wait_ge(s_mixp, g + 1)
                if g >= 2:
                    act.wait_ge(s_mix, g - 1)
                act.activation(s2c[:, p, :], bank[5][:, 256:512], ACT.Identity, bias=V["bv_c"])
                act.activation(th[:, p, :], bank[6][:, 0:256], ACT.Tanh, bias=bth, scale=0.5).then_inc(s_gate, 1)

            def D5(g):
                act.wait_ge(s_x3p, g + 1)
                if g >= 2:
                    act.wait_ge(s_lg, g - 1)
                act.activation(x3T[:, g % 2, :], bank[7][:, 0:256], ACT.Copy).then_inc(s_x3T, 1)

            for i in range(NG + 3):
                if i < NG:
                    A2(i)
                if 0 <= i - 2 < NG:
                    C2(i - 2)
                if i < NG:
                    A4(i)
                if 0 <= i - 1 < NG:
                    B5(i - 1)
                if 0 <= i - 3 < NG:
                    D5(i - 3)
                if i < NG:
                    B2(i)
                if i < NG:
                    if i == 0:
                        act.wait_ge(s_w01, 16)
                    act.activation(w01_h[:, i, :], w01_f[:, i, :], ACT.Copy).then_inc(s_wsp, 1)
            act.wait_ge(s_wts, 1)
            act.activation(wd[:, 1, :], wd[:, 0, :], ACT.Exp).then_inc(s_wts, 1)

            def F2(j, p):
                act.wait_ge(s_f1, j + 1)
                act.activation(xh[:, p, :], bank[0 + p][:, 0:128], ACT.Copy).then_inc(s_f2, 1)

            def F5(j, p):
                act.wait_ge(s_f4, j + 1)
                act.activation(sl[:, p, :], bank[2 + p][:, H:2 * H], ACT.Silu).then_inc(s_f5, 1)

            def F8(j, p):
                act.wait_ge(s_f7, j + 1)
                act.activation(aT[:, p, :], bank[4 + p][:, 0:H], ACT.Copy).then_inc(s_f8, 1)

            act.wait_ge(s_f1, 1)
            act.activation(xh[:, 0, :], bank[0][:, 0:128], ACT.Copy).then_inc(s_f2, 1)
            with act.Fori(0, (NBLK - 1) // 2) as i:
                for p in range(2):
                    F2(i * 2 + (p + 1), 1 - p)
                    F5(i * 2 + p, p)
                    F8(i * 2 + p, p)
            F5(NBLK - 1, (NBLK - 1) % 2)
            F8(NBLK - 1, (NBLK - 1) % 2)

        @block.vector
        def _(dve):
            steps = [0]

            def link(ins):
                steps[0] += 1
                ins.then_inc(s_v, 1)
                dve.wait_ge(s_v, steps[0])

            def norm_stats(n, g, done):
                p = g % 2
                for j in range(G):
                    ins = dve.bn_stats(stat[:, n, p, j, :], x_res[:, G * g + j, :])
                link(ins)
                for j in range(G):
                    ins = dve.bn_aggr(mv[:, n, p, j, :], stat[:, n, p, j, :])
                link(ins)
                dve.tensor_scalar(var[:, n, p, :], mv[:, n, p, :, 1], EPS, None, ALU.add).then_inc(done, 1)

            def L1(g):
                dve.wait_ge(s_x[g // 2], 16)
                norm_stats(0, g, s_var1)

            def L2(g):
                p = g % 2
                dve.wait_ge(s_rstd1, g + 1)
                if g >= 2:
                    dve.wait_ge(s_t, g - 1)
                for j in range(G):
                    ins = dve.tensor_scalar(xln[:, p, j, :], x_res[:, G * g + j, :], mv[:, 0, p, j, 0:1],
                                            rstd[:, 0, p, j:j + 1], ALU.subtract, ALU.mult)
                ins.then_inc(s_xln, 1)

            def B1(g):
                p = g % 2
                dve.wait_ge(s_sc, g + 1)
                dve.wait_ge(s_gs, 3 * (g + 1))
                dve.tensor_reduce(mx[:, p, 0:G], bank[2][:, 0:G * S].rearrange("p (g s) -> p g s", g=G), AX, ALU.max)
                link(dve.tensor_reduce(mx[0:S, p, G:2 * G], bank[2][0:S, 256:512].rearrange("p (g s) -> p g s", g=G),
                                       AX, ALU.max))
                link(dve.scalar_tensor_tensor(tot[:, p, :], mx[:, p, :], SCALE, sr[:, p, :], ALU.mult, ALU.add))
                dve.tensor_tensor(nb[:, p, :], sr[:, p, :], tot[:, p, :], ALU.subtract).then_inc(s_nb, 1)

            def B3(g):
                p = g % 2
                dve.wait_ge(s_exp, g + 1)
                link(dve.reciprocal(rcp[:, p, :], rs[:, p, :]))
                for j in range(G):
                    dve.tensor_scalar(P1[:, p, j, 0:S], P1[:, p, j, 0:S], rcp[:, p, j:j + 1], None, ALU.mult)
                for j in range(G):
                    ins = dve.tensor_scalar(P2[:, p, j, :], P2[:, p, j, :], rcp[0:S, p, G + j:G + j + 1], None, ALU.mult)
                ins.then_inc(s_prob, 1)

            def B7(g):
                dve.wait_ge(s_t, g + 1)
                if g >= 2:
                    dve.wait_ge(s_mixp, g - 1)
                dve.tensor_copy(TT[:, g % 2, :, :].rearrange("p a b -> p (a b)"), bank[4][:, :]).then_inc(s_tt, 1)

            def C3(g):
                p = g % 2
                dve.wait_ge(s_gate, g + 1)
                if g >= 2:
                    dve.wait_ge(s_mT, g - 1)
                link(dve.scalar_tensor_tensor(dif[:, p, :], bank[5][:, 0:256], V["bv_s"], s2c[:, p, :],
                                              ALU.add, ALU.subtract))
                link(dve.scalar_tensor_tensor(gd[:, p, :], th[:, p, :], 1.0, dif[:, p, :], ALU.add, ALU.mult))
                dve.scalar_tensor_tensor(mix[:, p, :], gd[:, p, :], 0.5, s2c[:, p, :],
                                         ALU.mult, ALU.add).then_inc(s_mix, 1)

            def C5(g):
                dve.wait_ge(s_mT, g + 1)
                xg = x_res[:, G * g:G * g + G, :].rearrange("p b d -> p (b d)")
                dve.scalar_tensor_tensor(xg, bank[6][:, 256:512], tgx, xg, ALU.mult, ALU.add).then_inc(s_x2, 1)

            def D1(g):
                dve.wait_ge(s_x2, g + 1)
                norm_stats(1, g, s_var2)

            def D3(g):
                p = g % 2
                dve.wait_ge(s_rstd2, g + 1)
                for j in range(G):
                    ins = dve.tensor_scalar(rows[:, G * g + j, 0, 0:D], x_res[:, G * g + j, :], mv[:, 1, p, j, 0:1],
                                            rstd[:, 1, p, j:j + 1], ALU.subtract, ALU.mult)
                link(ins)
                dve.tensor_copy(rows[:, G * g:G * g + G, 1, 0:D], rows[:, G * g:G * g + G, 0, 0:D]).then_inc(s_rows, 1)

            def choose(k, src, m_out):
                link(dve.tensor_reduce(m_out, src, AX, ALU.max))
                link(dve.tensor_tensor(eq[:, :, :], src, m_out.rearrange("p (q a) -> p q a", a=1).to_broadcast([128, Q, E]), ALU.is_equal))
                rev = cst[:, C_REV:C_REV + E].rearrange("p (a e) -> p a e", a=1).to_broadcast([128, Q, E])
                link(dve.tensor_tensor(key[:, :, :], eq[:, :, :], rev, ALU.mult))
                link(dve.tensor_reduce(km[:, :], key[:, :, :], AX, ALU.max))
                link(dve.tensor_tensor(oh[:, k, :, :], key[:, :, :],
                                       km[:, :].rearrange("p (q a) -> p q a", a=1).to_broadcast([128, Q, E]), ALU.is_equal))

            def R1(q):
                dve.wait_ge(s_lg, 2 * q + 2)
                gb = gate_bB.rearrange("p (a e) -> p a e", a=1).to_broadcast([128, Q, E])
                ins = dve.tensor_tensor(lg[:, :, :], bank[7][:, 256:256 + Q * E].rearrange("p (q e) -> p q e", q=Q), gb, ALU.add)
                link(ins)
                choose(0, lg[:, :, :], m1[:, q * Q:q * Q + Q])
                link(dve.scalar_tensor_tensor(lg2[:, :, :], oh[:, 0, :, :], -FAR, lg[:, :, :], ALU.mult, ALU.add))
                choose(1, lg2[:, :, :], m2[:, q * Q:q * Q + Q])
                dve.tensor_tensor(ohs[:, :, :], oh[:, 0, :, :], oh[:, 1, :, :], ALU.add).then_inc(s_oh, 1)
                dve.wait_ge(s_oh, q + 1)
                link(dve.tensor_reduce(ohq[:, :], ohs[:, :, :].rearrange("p q e -> p e q"), AX, ALU.add))
                link(dve.tensor_tensor(acc[:, q + 1, :], acc[:, q, :], ohq[:, :], ALU.add))

            def R3(q):
                dve.wait_ge(s_rank, q + 1)
                base = cst[:, C_BASE:C_BASE + E].rearrange("p (a e) -> p a e", a=1).to_broadcast([128, Q, E])
                link(dve.tensor_tensor(rk[:, :, :], bank[7][:, 320:320 + Q * E].rearrange("p (q e) -> p q e", q=Q), base, ALU.add))
                for k in range(2):
                    ins = dve.tensor_tensor(prod[:, k, :, :], oh[:, k, :, :], rk[:, :, :], ALU.mult)
                link(ins)
                with nc.allow_low_precision(reason="whole numbers below 2**24, summed in float32"):
                    dve.tensor_reduce(pos[:, q, :, :], prod[:, :, :, :], AX, ALU.add).then_inc(s_pos, 1)

            dve.wait_ge(s_pack, 16)
            for i, n in enumerate(("bq_c", "bq_s")):
                ins = dve.tensor_copy(bq_rep[:, i, :], V[n].to_broadcast([128, D]))
            link(ins)
            L1(0)
            L2(0)
            dve.wait_ge(s_dest, 16)
            for k in range(2):
                dve.tensor_copy(rows[:, :, k, D:D + 1].bitcast(I32).rearrange("p b a -> p (b a)"), dest[:, k, :])
                dve.memset(rows[:, :, k, D + 1:ROW], 0.0)
            dve.wait_ge(s_folded, 18)
            dve.wait_ge(s_setup, 9)

            for i in range(NG + 3):
                if 0 <= i - 1 < NG:
                    B3(i - 1)
                if 0 <= i - 3 < NG:
                    D1(i - 3)
                if 0 <= i - 2 < NG:
                    C3(i - 2)
                if 0 <= i - 3 < NG:
                    D3(i - 3)
                if 0 <= i - 1 < NG:
                    B7(i - 1)
                if 0 <= i - 2 < NG:
                    C5(i - 2)
                if i + 1 < NG:
                    L1(i + 1)
                if i < NG:
                    B1(i)
                if i + 1 < NG:
                    L2(i + 1)
                if 0 <= i - 3 < NG and i % 2 == 0:
                    R1((i - 3) // 2)
                    R3((i - 3) // 2)
                if i < NG:
                    dve.wait_ge(s_wsp, i + 1)
                    dve.tensor_tensor(w01_l[:, i, :], w01_f[:, i, :], w01_h[:, i, :].bitcast(F32),
                                      ALU.subtract).then_inc(s_wsl, 1)
                if i == 0:
                    dve.wait_ge(s_b1, 16)
                    b1f = b1_s[:, :, :].rearrange("p e h -> p (e h)")
                    link(dve.memset(b1f, 0.0))
                    for n in range(3):
                        r = slice(32 * n, 32 * n + 1)
                        for m in range(n + 1):
                            src = b1_p if m == 0 else b1_r
                            link(dve.tensor_copy(b1f[r, :], src[r, :]))
                            if m < n:
                                link(dve.tensor_tensor(b1_r[r, :], src[r, :], b1f[r, :], ALU.subtract))
                    dve.sem_inc(s_b1s, 1)

            dve.wait_ge(s_cnt, 1)
            dve.tensor_copy(nrow_i[:, :], bank[3][0:1, 8:8 + E]).then_inc(s_nrow, 1)
            link(dve.tensor_scalar(nbk_i[:, :], bank[3][0:E, 0:1], 1.0 / L, (L - 1.0) / L - 0.498, ALU.mult, ALU.add))
            dve.tensor_copy(nbk[:, :], nbk_i[:, :]).then_inc(s_tabv, 1)
            dve.wait_ge(s_tab, 1)
            link(dve.tensor_copy(bcum[:, :], bank[3][0:E, 1:2]))
            dve.tensor_scalar(cmp[:, :], cst[0:E, C_JS:C_JS + NBLK], bcum[:, 0:1], None, ALU.is_ge).then_inc(s_tabv, 1)
            dve.wait_ge(s_tab, 2)
            link(dve.tensor_copy(es[:, :, :].rearrange("p a j -> p (a j)"), bank[3][0:1, 16:16 + 2 * NBLK]))
            dve.tensor_scalar(e_i[:, :], es[:, 0, :], E - 1.0, None, ALU.min)
            dve.tensor_scalar(off[:, :], es[:, 0, :], float(LIST), None, ALU.mult).then_inc(s_tabv, 1)
            dve.wait_ge(s_tabv, 3)
            link(dve.scalar_tensor_tensor(off[:, :], es[:, 1, :], -float(L), off[:, :], ALU.mult, ALU.add))
            link(dve.scalar_tensor_tensor(r_i[:, :], cst[0:1, C_JS:C_JS + NBLK], float(L), off[:, :], ALU.mult, ALU.add))
            dve.sem_inc(s_table, 1)
            link(dve.tensor_tensor(wd[:, 0, :], m2[:, :], m1[:, :], ALU.subtract))
            dve.sem_inc(s_wts, 1)
            dve.wait_ge(s_wts, 2)
            link(dve.tensor_scalar(wd[:, 2, :], wd[:, 1, :], 1.0, None, ALU.add))
            link(dve.reciprocal(wd[:, 3, :], wd[:, 2, :]))
            link(dve.tensor_scalar(wd[:, 0, :], wd[:, 3, :], tgf, None, ALU.mult))
            link(dve.tensor_tensor(wd[:, 1, :], wd[:, 1, :], wd[:, 0, :], ALU.mult))

            dve.wait_ge(s_b0, 16)
            dve.wait_ge(s_b2, 16)

            def F3(j, p):
                dve.wait_ge(s_f2, j + 1)
                dve.tensor_tensor(xl[:, p, :], bank[0 + p][:, 0:128], xh[:, p, :].bitcast(F32), ALU.subtract).then_inc(s_f3, 1)

            def F6(j, p):
                e = dve.value_load(e_i[0:1, bass.ds(j, 1)], min_val=0, max_val=E - 1)
                dve.wait_ge(s_f5, j + 1)
                b0e = b0_B[:, bass.ds(e, 1), :].rearrange("p a h -> p (a h)")
                dve.tensor_tensor(hb[:, p, :], bank[2 + p][:, 0:H], b0e, ALU.add).then_inc(s_f6a, 1)
                dve.wait_ge(s_f6a, j + 1)
                dve.tensor_tensor(ab[:, p, :], hb[:, p, :], sl[:, p, :], ALU.mult).then_inc(s_f6, 1)
                return e

            def F10(j, p, b, e, first=False):
                dve.wait_ge(s_f9, j + 1)
                if not first:
                    dve.wait_ge(s_sc2[b], 16 * ((j - b) // NX) if isinstance(j, int) else 16 * first_i[0])
                b2e = b2_B[:, bass.ds(e, 1), :].rearrange("p a d -> p (a d)")
                dve.tensor_tensor(yb[:, b, :], bank[6 + p][:, 0:D], b2e, ALU.add).then_inc(s_f10, 1)

            first_i = [None]
            F3(0, 0)
            for j in range(NX):
                F3(j + 1, (j + 1) % 2)
                e = F6(j, j % 2)
                F10(j, j % 2, j, e, first=True)
            with dve.Fori(0, NBLK // NX - 1) as i:
                for b in range(NX):
                    j = i * NX + (b + NX)
                    F3(j + 1, (b + 1) % 2)
                    e = F6(j, b % 2)
                    first_i[0] = i + 1
                    F10(j, b % 2, b, e)
            for j in range(NBLK // NX * NX, NBLK):
                if j + 1 < NBLK:
                    F3(j + 1, (j + 1) % 2)
                e = F6(j, j % 2)
                F10(j, j % 2, j % NX, e)

            for q in range(NQ):
                dve.wait_ge(s_yin[q], 32)
                for j in range(Q):
                    t = q * Q + j
                    ins = dve.scalar_tensor_tensor(o1[:, q, j, :], yin[:, q, 0, j, :], wd[:, 0, t:t + 1],
                                                   x_res[:, t, :], ALU.mult, ALU.add)
                link(ins)
                for j in range(Q):
                    t = q * Q + j
                    ins = dve.scalar_tensor_tensor(x_res[:, t, :], yin[:, q, 1, j, :], wd[:, 1, t:t + 1],
                                                   o1[:, q, j, :], ALU.mult, ALU.add)
                ins.then_inc(s_fin, 1)

        @block.tensor
        def _(pe):
            pe.wait_ge(s_pack, 16)
            pe.wait_ge(s_v, 1)
            bqr_c, bqr_s = bq_rep[:, 0, :], bq_rep[:, 1, :]
            pe.matmul(bank[0][:, 0:D], W["Wk_s"], W["Wq_c"], start=True, stop=True)
            pe.matmul(bank[0][:, D:2 * D], W["Wq_s"], W["Wk_c"], start=True, stop=True)
            pe.matmul(bank[0][:, 2 * D:3 * D], W["Wk_s"], bqr_c, start=True, stop=True).then_inc(s_fold, 1)
            pe.matmul(bank[1][:, 0:D], W["Wv_s"], W["WgT_1"], start=True, stop=True)
            pe.matmul(bank[1][:, D:2 * D], W["Wv_c"], W["WgT_2"], start=True, stop=True).then_inc(s_fold, 1)
            for i, (a, b) in enumerate(((W["Wq_c"], V["bk_s"]), (W["Wk_c"], V["bq_s"]), (W["Wq_s"], V["bk_c"]),
                                        (bqr_c, V["bk_s"]), (bqr_s, V["bk_c"]))):
                pe.matmul(bank[2][:, i:i + 1], a, b, start=True, stop=True)
            pe.wait_ge(s_cst, 16)
            pe.matmul(bank[2][:, 5:6], W["WgT_1"], V["bv_s"], start=True, stop=False)
            pe.matmul(bank[2][:, 5:6], W["WgT_2"], V["bv_c"], start=False, stop=False)
            pe.matmul(bank[2][:, 5:6], ident, V["bg"], start=False, stop=True).then_inc(s_fold, 1)
            pe.wait_ge(s_folded, 14)

            def A1(g):
                p = g % 2
                pe.wait_ge(s_c[p], 16 * (g // 2 + 1))
                if g >= 1:
                    pe.wait_ge(s_tT, g)
                pe.wait_ge(s_xln, g + 1)
                for j in range(G):
                    pe.transpose(bank[0][:, G * L + j * S:G * L + j * S + S], c_in[:, p, j, :], cst[0:S, C_ID:C_ID + S])
                for j in range(G):
                    ins = pe.transpose(bank[0][:, j * L:j * L + L], xln[:, p, j, :], ident)
                ins.then_inc(s_tp, 1)

            def A3(g):
                p = g % 2
                pe.wait_ge(s_tT, g + 1)
                if g >= 1:
                    pe.wait_ge(s_gs, 3 * g)
                cT = tT[:, p, G * L:G * L + G * S]
                pe.matmul(bank[1][:, 0:G * S], A1T[:, :], cT, start=True, stop=True)
                pe.matmul(bank[1][:, G * S:2 * G * S], A2T[:, :], cT, start=True, stop=True)
                for j in range(G):
                    ins = pe.matmul(bank[1][0:S, 2 * G * S + j:2 * G * S + j + 1], cT[:, j * S:j * S + S], u2,
                                    start=True, stop=True)
                ins.then_inc(s_g, 1)

            def A5(g):
                p = g % 2
                pe.wait_ge(s_gs, 3 * (g + 1))
                if g >= 1:
                    pe.wait_ge(s_exp, g)
                cT = tT[:, p, G * L:G * L + G * S]
                pe.matmul(bank[2][:, 0:G * S], U1[:, :], cT, start=True, stop=False, skip_group_check=True)
                for j in range(G):
                    pe.matmul(bank[2][:, j * S:j * S + S], tT[:, p, j * L:j * L + L], Gs[:, p, 0, j * S:j * S + S],
                              start=False, stop=(j == G - 1), skip_group_check=True)
                for j in range(G):
                    ins = pe.matmul(bank[2][0:S, 256 + j * L:256 + j * L + L], Gs[:, p, 1, j * S:j * S + S],
                                    tT[:, p, j * L:j * L + L], start=True, stop=True)
                ins.then_inc(s_sc, 1)

            def B4(g):
                p = g % 2
                pe.wait_ge(s_prob, g + 1)
                if g >= 1:
                    pe.wait_ge(s_ptc, g)
                for j in range(G):
                    pe.transpose(bank[3][:, j * L:j * L + L], P1[:, p, j, :], ident)
                for j in range(G):
                    ins = pe.matmul(bank[3][:, 256 + j * L:256 + j * L + L], P2[:, p, j, :], interpT, start=True, stop=True)
                ins.then_inc(s_pt, 1)

            def B6(g):
                p = g % 2
                pe.wait_ge(s_ptc, g + 1)
                if g >= 1:
                    pe.wait_ge(s_tt, g)
                for j in range(G):
                    pe.matmul(bank[4][:, j * L:j * L + L], c_in[:, p, j, :], PT[0:S, p, 0, j, :], start=True, stop=True)
                for j in range(G):
                    ins = pe.matmul(bank[4][:, 256 + j * L:256 + j * L + L], xln[:, p, j, :], PT[:, p, 1, j, :],
                                    start=True, stop=True)
                ins.then_inc(s_t, 1)

            def C1(g):
                p = g % 2
                pe.wait_ge(s_tt, g + 1)
                if g >= 1:
                    pe.wait_ge(s_mix, g)
                    pe.wait_ge(s_x2, g)
                t1, t2 = TT[:, p, 0, :], TT[:, p, 1, :]
                pe.matmul(bank[5][:, 0:256], W["WvT_s"], t1, start=True, stop=True)
                pe.matmul(bank[5][:, 256:512], W["WvT_c"], t2, start=True, stop=True)
                pe.matmul(bank[6][:, 0:256], AG1T[:, :], t1, start=True, stop=False)
                pe.matmul(bank[6][:, 0:256], AG2T[:, :], t2, start=False, stop=True).then_inc(s_mixp, 1)

            def C4(g):
                p = g % 2
                pe.wait_ge(s_mix, g + 1)
                for j in range(G):
                    ins = pe.transpose(bank[6][:, 256 + j * L:256 + j * L + L], mix[:, p, j * L:j * L + L], ident)
                ins.then_inc(s_mT, 1)

            def D4(g):
                pe.wait_ge(s_rows, g + 1)
                if g >= 1:
                    pe.wait_ge(s_x3T, g)
                    if g % 2 == 0:
                        pe.wait_ge(s_pos, g // 2)
                for j in range(G):
                    ins = pe.transpose(bank[7][:, j * L:j * L + L], rows[:, G * g + j, 0, 0:D], ident)
                ins.then_inc(s_x3p, 1)

            def D6(g):
                p = g % 2
                pe.wait_ge(s_x3T, g + 1)
                for j in range(G):
                    o = 256 + (G * p + j) * E
                    ins = pe.matmul(bank[7][:, o:o + E], x3T[:, p, j * L:j * L + L], gate_wT, start=True, stop=True)
                ins.then_inc(s_lg, 1)

            def R2(q):
                pe.wait_ge(s_oh, q + 1)
                R = bank[7][:, 320:320 + Q * E].rearrange("p (q e) -> p q e", q=Q)
                pe.matmul(R, one16[:, :], acc[:, q, :].rearrange("p (a e) -> p a e", a=1).to_broadcast([128, Q, E]),
                          start=True, stop=False, skip_group_check=True)
                for j in range(Q - 1):
                    pe.matmul(R[:, j + 1:Q, :], one16[:, :],
                              ohs[:, j, :].rearrange("p (a e) -> p a e", a=1).to_broadcast([128, Q - 1 - j, E]),
                              start=False, stop=False, skip_group_check=True)
                pe.matmul(R, lt16[:, :], ohs[:, :, :], start=False, stop=True, skip_group_check=True).then_inc(s_rank, 1)

            for i in range(NG + 3):
                if i < NG:
                    A1(i)
                if 0 <= i - 2 < NG:
                    C1(i - 2)
                if 0 <= i - 1 < NG:
                    B4(i - 1)
                if i < NG:
                    A3(i)
                if 0 <= i - 3 < NG:
                    D4(i - 3)
                if 0 <= i - 1 < NG:
                    B6(i - 1)
                if i < NG:
                    A5(i)
                if 0 <= i - 2 < NG:
                    C4(i - 2)
                if 0 <= i - 3 < NG:
                    D6(i - 3)
                if 0 <= i - 3 < NG and i % 2 == 0:
                    R2((i - 3) // 2)

            pe.wait_ge(s_pos, NQ)
            pe.matmul(bank[3][0:E, 0:1], acc[:, NQ, :], one16[:, 0:1], start=True, stop=True)
            pe.matmul(bank[3][0:1, 8:8 + E], one16[:, 0:1], acc[:, NQ, :], start=True, stop=True).then_inc(s_cnt, 1)
            pe.wait_ge(s_tabv, 1)
            pe.wait_ge(s_nrow, 1)
            pe.matmul(bank[3][0:E, 1:2], cst[0:E, C_UT:C_UT + E], nbk[:, :], start=True, stop=True).then_inc(s_tab, 1)
            pe.wait_ge(s_tabv, 2)
            pe.matmul(bank[3][0:1, 16:16 + NBLK], ones[0:E, 0:1], cmp[:, :], start=True, stop=True)
            pe.matmul(bank[3][0:1, 16 + NBLK:16 + 2 * NBLK], nbk[:, :], cmp[:, :], start=True, stop=True).then_inc(s_tab, 1)

            pe.wait_ge(s_wsl, E)
            pe.wait_ge(s_w2, 16)
            pe.wait_ge(s_b1s, 1)
            pe.wait_ge(s_table, 1)

            def F1(j, p, b, n):
                pe.wait_ge(s_xb[b], n)
                pe.transpose(bank[0 + p][:, 0:128], xb[:, b, 0:D], ident).then_inc(s_f1, 1)

            def F4(j, p):
                e = pe.value_load(e_i[0:1, bass.ds(j, 1)], min_val=0, max_val=E - 1)
                pe.wait_ge(s_f3, j + 1)
                wh = w01_h[:, bass.ds(e, 1), :].rearrange("p a n -> p (a n)")
                wl = w01_l[:, bass.ds(e, 1), :].rearrange("p a n -> p (a n)")
                pe.matmul(bank[2 + p][:, :], xh[:, p, :], wh, start=True, stop=False, skip_group_check=True)
                pe.matmul(bank[2 + p][:, :], xh[:, p, :], wl, start=False, stop=False, skip_group_check=True)
                pe.matmul(bank[2 + p][:, :], xl[:, p, :], wh, start=False, stop=False, skip_group_check=True)
                b1e = b1_s[0:65, bass.ds(e, 1), :].rearrange("p a n -> p (a n)")
                pe.matmul(bank[2 + p][:, H:2 * H], sel3[0:65, :], b1e, start=False, stop=True,
                          skip_group_check=True).then_inc(s_f4, 1)
                return e

            def F7(j, p):
                pe.wait_ge(s_f6, j + 1)
                for h in range(2):
                    ins = pe.transpose(bank[4 + p][:, h * 128:h * 128 + 128], ab[:, p, h * 128:h * 128 + 128], ident)
                ins.then_inc(s_f7, 1)

            def F9(j, p, e):
                pe.wait_ge(s_f8, j + 1)
                for h in range(2):
                    ins = pe.matmul(bank[6 + p][:, 0:D], aT[:, p, h * 128:h * 128 + 128],
                                    w2_f[:, bass.ds(e, 1), h, :].rearrange("p a n -> p (a n)"),
                                    start=(h == 0), stop=(h == 1))
                ins.then_inc(s_f9, 1)

            F1(0, 0, 0, 16)
            F1(1, 1, 1, 16)
            e0 = F4(0, 0)
            def e_of(j):
                return pe.value_load(e_i[0:1, bass.ds(j, 1)], min_val=0, max_val=E - 1)

            for j in range(2):
                F4(j + 1, (j + 1) % 2)
                F7(j, j % 2)
                F1(j + 2, j % 2, (j + 2) % NX, 16)
                F9(j, j % 2, e_of(j))
            with pe.Fori(0, NBLK // NX - 1) as i:
                for b in range(NX):
                    j = i * NX + (b + 2)
                    F4(j + 1, (b + 1) % 2)
                    F7(j, b % 2)
                    F1(j + 2, b % 2, b, 16 * (i + 2))
                    F9(j, b % 2, e_of(j))
            for j in range((NBLK // NX - 1) * NX + 2, NBLK):
                if j + 1 < NBLK:
                    F4(j + 1, (j + 1) % 2)
                F7(j, j % 2)
                if j + 2 < NBLK:
                    F1(j + 2, j % 2, (j + 2) % NX, 16 * ((j + 2) // NX + 1))
                F9(j, j % 2, e_of(j))


def kernel(**inputs):
    import numpy as np
    import concourse.bacc as bacc
    from concourse.bass_utils import run_bass_kernel_spmd

    a = {k: np.asarray(v) for k, v in inputs.items()}
    f = np.float32

    def xa(n):
        return a["L0_xattn_" + n]

    def col(v):
        return np.broadcast_to(v.reshape(-1, 1), (128, 1))

    wgT = xa("Wg").T
    wpack = np.concatenate(
        [xa("Wq_c"), xa("Wk_s"), xa("Wq_s"), xa("Wk_c"), xa("Wv_s"), xa("Wv_c"), xa("Wv_s").T, xa("Wv_c").T,
         wgT[0:D], wgT[D:2 * D]]
        + [col(xa(n)) for n in ("bq_c", "bk_s", "bq_s", "bk_c", "bv_s", "bv_c", "bg")]
        + [col(a["g_xattn"]), col(a["g_ffn"]), a["L0_ffn_gate_w"].T,
           np.broadcast_to(a["L0_ffn_gate_b"].reshape(1, E), (128, E))], axis=1)
    w01 = np.concatenate([a["L0_ffn_w0"].transpose(2, 0, 1), a["L0_ffn_w1"].transpose(2, 0, 1)], axis=2)
    w2 = a["L0_ffn_w2"].reshape(E, D, 2, 128).transpose(3, 0, 2, 1)
    b1 = np.broadcast_to(a["L0_ffn_b1"].reshape(1, E * H), (128, E * H))

    consts = np.zeros((128, N_CONST), f)
    consts[:, C_ID:C_ID + 128] = np.eye(128)
    at = np.clip((np.arange(L, dtype=f) + f(0.5)) * f(S / L) - f(0.5), f(0), f(S - 1))
    lo = np.floor(at).astype(np.int32)
    w = at - lo.astype(f)
    for i in range(L):
        consts[lo[i], C_IT + i] += f(1) - w[i]
        consts[min(lo[i] + 1, S - 1), C_IT + i] += w[i]
    consts[:, C_LT:C_LT + 128] = np.triu(np.ones((128, 128)), 1)
    consts[0:E, C_UT:C_UT + E] = np.triu(np.ones((E, E)))
    consts[:, C_REV:C_REV + E] = E - np.arange(E)
    consts[:, C_BASE:C_BASE + E] = np.arange(E) * LIST
    consts[:, C_JS:C_JS + NBLK] = np.arange(NBLK)
    tok = np.arange(B)[None, :] * L + np.arange(128)[:, None]
    dests = np.stack([tok, T + tok], axis=1).astype(np.int32)
    pads = np.zeros((128, E + IDLE, ROW), f)
    pads[:, :, D] = (2 * T + np.arange(E + IDLE)[None, :] * L + np.arange(128)[:, None]).astype(np.int32).view(f)

    feeds = {"x": a["x"], "ctx_in": a["ctx_1024"], "wpack": wpack, "w01": w01, "w2": w2, "b0": a["L0_ffn_b0"],
             "b1": b1, "b2": a["L0_ffn_b2"], "consts": consts, "dests": dests, "pads": pads}
    nc = bacc.Bacc("TRN2", target_bir_lowering=False, num_devices=1)
    arrays, args = {}, []
    for name, v in feeds.items():
        v = np.ascontiguousarray(v)
        arrays[f"in_{name}"] = v
        args.append(nc.dram_tensor(f"in_{name}", v.shape, mybir.dt.from_np(v.dtype), kind="ExternalInput").ap())
    out = nc.dram_tensor("out", (B, L, D), F32, kind="ExternalOutput").ap()
    flamingo_kernel(nc, *args, out)
    r = run_bass_kernel_spmd(nc, [arrays], core_ids=[0])
    return r.results[0]["out"]
```

```python
from contextlib import ExitStack

import concourse.bass as bass
from concourse import mybir

F32 = mybir.dt.float32
F32R = mybir.dt.float32r
BF16 = mybir.dt.bfloat16
I32 = mybir.dt.int32
ALU = mybir.AluOpType
ACT = mybir.ActivationFunctionType
AX = mybir.AxisListType.X

B = 16
L = 128
D = 128
S = 77
E = 8
H = 256
G = 2
NG = B // G
NQ = NG // 2
T = B * L
SCALE = 1.0 / float(D) ** 0.5
EPS = 1e-5
FAR = 1.0e30

LIST = T + L
NBLK = 2 * T // L + E - 1
NX = 8
FIRST = NX + 2
LOOPS = (NBLK - 2 - FIRST) // NX
IDLE = E - 1
ROW = D + 4
XS_ROWS = E * LIST + IDLE * L
Y_ROWS = 2 * T + (E + IDLE) * L

W_NAMES = ["Wq_c", "Wk_s", "Wq_s", "Wk_c", "Wv_s", "Wv_c", "WvT_s", "WvT_c", "WgT_1", "WgT_2"]
V_NAMES = ["bq_c", "bk_s", "bq_s", "bk_c", "bv_s", "bv_c", "bg", "g_x", "g_f"]
N_PACK = len(W_NAMES) * D + len(V_NAMES) + 2 * E
C_ID, C_IT, C_LT, C_UT, C_REV, C_BASE, C_JS, C_LIST = 0, 128, 256, 384, 392, 400, 408, 408 + NBLK
N_CONST = C_LIST + E


def flamingo_kernel(nc, x, ctx_in, wpack, w01, w2, b0, b1, b2, consts, dests, pads, out):
    xs = nc.dram_tensor("xs_lists", (XS_ROWS, ROW), F32).ap()
    ys = nc.dram_tensor("y_rows", (Y_ROWS, D), F32).ap()
    stack = ExitStack()
    with stack:
        def sb(name, shape, dt=F32):
            return stack.enter_context(nc.sbuf_tensor(name, shape, dt))

        def sem(name):
            return stack.enter_context(nc.semaphore(name))

        x_res = sb("x_res", [128, B, D])
        c_in = sb("c_in", [S, B, D])
        pack = sb("pack", [128, N_PACK])
        cst = sb("cst", [128, N_CONST])
        dest = sb("dest", [128, 2, B], I32)
        pad = sb("pad", [128, E + IDLE, ROW])
        pad_i = sb("pad_i", [128, E + IDLE])
        W = {n: pack[:, i * D:(i + 1) * D] for i, n in enumerate(W_NAMES)}
        V = {n: pack[:, len(W_NAMES) * D + i:len(W_NAMES) * D + i + 1] for i, n in enumerate(V_NAMES)}
        o = len(W_NAMES) * D + len(V_NAMES)
        gate_wT, gate_bB = pack[:, o:o + E], pack[:, o + E:o + 2 * E]
        ident = cst[:, C_ID:C_ID + 128]
        interpT = cst[0:S, C_IT:C_IT + L]

        A1T = sb("A1T", [128, D])
        A2T = sb("A2T", [128, D])
        U1 = sb("U1", [128, D])
        AG1T = sb("AG1T", [128, D])
        AG2T = sb("AG2T", [128, D])
        bq_rep = sb("bq_rep", [128, 2, D])
        vec = sb("vec", [128, 8])
        g1b, g2b, u2, k1s, k2s, bth, tgx, tgf = (vec[:, i:i + 1] for i in range(8))
        lt16 = sb("lt16", [128, 128], BF16)
        one16 = sb("one16", [128, 128], BF16)
        ones = sb("ones", [128, 8])

        stat = sb("stat", [128, 2, 2, G, 6])
        mv = sb("mv", [128, 2, 2, G, 2])
        var = sb("var", [128, 2, 2, G])
        rstd = sb("rstd", [128, 2, 2, G])
        halfn = sb("halfn", [128, G])
        xln = sb("xln", [128, B, D])
        tT = sb("tT", [128, 2, G * L + G * S])
        Gs = sb("Gs", [128, 2, 2, G * S])
        sr = sb("sr", [128, 2, 2 * G])
        mx = sb("mx", [128, 2, 2 * G])
        tot = sb("tot", [128, 2, 2 * G])
        nb = sb("nb", [128, 2, 2 * G])
        rs = sb("rs", [128, 2, 2 * G])
        rcp = sb("rcp", [128, 2, 2 * G])
        P1 = sb("P1", [128, 2, G, 128])
        P2 = sb("P2", [S, 2, G, 128])
        PT = sb("PT", [128, 2, 2, G, 128])
        TT = sb("TT", [128, 2, 2, G * L])
        s2c = sb("s2c", [128, 2, G * L])
        th = sb("th", [128, 2, G * L])
        dif = sb("dif", [128, 2, G * L])
        gd = sb("gd", [128, 2, G * L])
        mix = sb("mix", [128, 2, G * L])
        rows = sb("rows", [128, B, 2, ROW])
        x3T = sb("x3T", [128, 2, G * L])

        Q = 2 * G
        lg = sb("lg", [128, Q, E])
        lg2 = sb("lg2", [128, Q, E])
        m1 = sb("m1", [128, B])
        m2 = sb("m2", [128, B])
        eq = sb("eq", [128, Q, E])
        key = sb("key", [128, Q, E])
        km = sb("km", [128, Q])
        oh = sb("oh", [128, 2, Q, E])
        ohs = sb("ohs", [128, Q, E], BF16)
        ohq = sb("ohq", [128, E])
        acc = sb("acc", [128, NQ + 1, E], BF16)
        rk = sb("rk", [128, Q, E])
        prod = sb("prod", [128, 2, Q, E])
        pos = sb("pos", [128, NQ, 2, Q], I32)

        nrow = sb("nrow", [1, E])
        nrow_i = sb("nrow_i", [1, E], I32)
        nbk_i = sb("nbk_i", [E, 1], I32)
        nbk = sb("nbk", [E, 1])
        bcum = sb("bcum", [E, 1])
        cmp = sb("cmp", [E, NBLK])
        es = sb("es", [1, 2, NBLK])
        e_i = sb("e_i", [1, NBLK], I32)
        off = sb("off", [1, NBLK])
        r_i = sb("r_i", [1, NBLK], I32)
        wd = sb("wd", [128, 4, B])

        w01_f = sb("w01_f", [128, E, 2 * H])
        w01_h = sb("w01_h", [128, E, 2 * H], F32R)
        w01_l = sb("w01_l", [128, E, 2 * H], F32R)
        w2_f = sb("w2_f", [128, E, 2, D])
        b0_B = sb("b0_B", [128, E, H])
        b2_B = sb("b2_B", [128, E, D])
        b1_p = sb("b1_p", [128, E * H // 128])
        b1_r = sb("b1_r", [128, 2, E * H // 128])
        b1_3 = sb("b1_3", [128, 3, E * H // 128], BF16)
        b1_s = sb("b1_s", [3, E, H], BF16)
        
        xb = sb("xb", [128, NX, ROW])
        xh = sb("xh", [128, 2, 128], F32R)
        xl = sb("xl", [128, 2, 128], F32R)
        sl = sb("sl", [128, 2, H])
        hb = sb("hb", [128, 2, H])
        ab = sb("ab", [128, 2, H])
        aT = sb("aT", [128, 2, H])
        yb = sb("yb", [128, NX, D])
        yin = sb("yin", [128, NQ, 2, Q, D])
        o1 = sb("o1", [128, NQ, Q, D])

        bank = [stack.enter_context(nc.psum_tensor(f"bank{i}", [128, 512], F32)) for i in range(8)]

        s_pack, s_cst, s_dest, s_pad, s_w2, s_b0, s_b1, s_b2 = (
            sem("in_" + n) for n in "pack cst dest pad w2 b0 b1 b2".split())
        s_w01 = [sem(f"in_w01_{h}") for h in range(2)]
        s_x = [sem(f"in_x{q}") for q in range(NQ)]
        s_c = [sem(f"in_c{h}") for h in range(2)]
        s_setup = sem("setup_memsets")
        s_fold = sem("fold_products")
        s_folded = sem("folded_weights")
        s_var1, s_rstd1, s_xln = sem("var1"), sem("rstd1"), sem("xln")
        s_tp, s_tT, s_g, s_gs, s_sc = sem("xc_transposed"), sem("xc_T_in_sbuf"), sem("G_made"), sem("G_in_sbuf"), sem("scores")
        s_nb, s_exp, s_prob = sem("neg_max"), sem("exps"), sem("probs")
        s_pt, s_ptc, s_t, s_tt = sem("probs_T"), sem("probs_T_in_sbuf"), sem("t_products"), sem("t_in_sbuf")
        s_mixp, s_gate, s_mix, s_mT, s_x2 = sem("mix_products"), sem("gate_tanh"), sem("mix"), sem("mix_T"), sem("x2")
        s_var2, s_rstd2, s_rows = sem("var2"), sem("rstd2"), sem("rows_ready")
        s_x3p, s_x3T, s_lg = sem("x3_transposed"), sem("x3T_in_sbuf"), sem("logits")
        s_lgr = sem("logits_read")
        s_oh, s_rank, s_rkr, s_pos = sem("one_hots"), sem("ranks"), sem("ranks_read"), sem("positions")
        s_scat = sem("scattered")
        s_cnt, s_nrow, s_padw = sem("counts"), sem("counts_in_sbuf"), sem("pads_written")
        s_tab = sem("table_products")
        s_tabv = sem("table_steps")
        s_table = sem("tables_ready")
        s_wsp = sem("w01_hi")
        s_wsl = sem("w01_lo")
        s_b1s = sem("b1_split")
        s_b1r = sem("b1_rows")
        s_x0 = sem("in_x_first_group")
        s_padm = sem("pads_made")
        s_padz = sem("pads_zero")
        s_xb = [sem(f"block_in{b}") for b in range(NX)]
        s_sc2 = [sem(f"block_out{b}") for b in range(NX)]
        s_f1, s_f2, s_f3, s_f4, s_f5, s_f6 = (sem(n) for n in "blk_xT blk_hi blk_lo blk_h blk_silu blk_act".split())
        s_f6a = sem("blk_h0")
        s_f7, s_f8, s_f9, s_f10 = (sem(n) for n in "blk_aT blk_aT_in_sbuf blk_y blk_y_in_sbuf".split())
        s_seen = sem("block_seen")
        s_yin = [sem(f"y_in{q}") for q in range(NQ)]
        s_o1 = sem("first_choice_added")
        s_fin = sem("final_rows")
        s_out = sem("stored")
        s_wts = sem("choice_weights")
        s_v = sem("vector_step")
        s_a = sem("scalar_step")

        block = stack.enter_context(nc.Block())

        xv = x.rearrange("b l d -> l b d")
        cv = ctx_in.rearrange("b l d -> l b d")
        ov = out.rearrange("b l d -> l b d")
        yv = ys[0:2 * T, :].rearrange("(k b l) d -> l k b d", k=2, b=B)

        @block.sync
        def _(sp):
            x0 = x_res[:, 0:Q, :]
            sp.dma_start(x0[:, 0:G, :], xv[:, 0:G, :]).then_inc(s_x0, 16)
            sp.dma_start(pack[:, :], wpack).then_inc(s_pack, 16)
            sp.dma_start(c_in[:, 0:Q, :], cv[:, 0:Q, :]).then_inc(s_c[0], 16)
            sp.dma_start(x0[:, G:Q, :], xv[:, G:Q, :]).then_inc(s_x[0], 16)
            sp.dma_start(x_res[:, Q:2 * Q, :], xv[:, Q:2 * Q, :]).then_inc(s_x[1], 16)
            sp.dma_start(c_in[:, Q:B, :], cv[:, Q:B, :]).then_inc(s_c[1], 16)
            for q in range(2, NQ):
                sp.dma_start(x_res[:, q * Q:q * Q + Q, :], xv[:, q * Q:q * Q + Q, :]).then_inc(s_x[q], 16)
            sp.dma_start(w01_f[:, 0:E // 2, :], w01[:, 0:E // 2, :]).then_inc(s_w01[0], 16)
            sp.dma_start(w01_f[:, E // 2:E, :], w01[:, E // 2:E, :]).then_inc(s_w01[1], 16)
            sp.dma_start(w2_f[:, :, :, :], w2).then_inc(s_w2, 16)
            sp.dma_start(b0_B[:, :, :], b0.partition_broadcast(128)).then_inc(s_b0, 16)
            sp.dma_start(b2_B[:, :, :], b2.partition_broadcast(128)).then_inc(s_b2, 16)
            sp.wait_ge(s_b1s, 1)
            for n in range(3):
                sp.dma_start(b1_s[n:n + 1, :, :], b1_3[:, n, :]).then_inc(s_b1r, 16)
            sp.wait_ge(s_padm, 1)
            sp.dma_start(xs[E * LIST:XS_ROWS, :].rearrange("(i p) d -> p i d", p=L),
                         pad[:, E:E + IDLE, :]).then_inc(s_padw, 16)
            sp.wait_ge(s_nrow, 1)
            for e in range(E):
                n = sp.value_load(nrow_i[0:1, e:e + 1], min_val=0, max_val=T)
                sp.dma_start(xs[bass.ds(n + e * LIST, L), :], pad[:, e, :]).then_inc(s_padw, 16)
            sp.wait_ge(s_table, 1)
            sp.wait_ge(s_padw, 16 * (E + 1))
            sp.wait_ge(s_scat, 16 * 2 * B)

            def load_block(j, b):
                r = sp.value_load(r_i[0:1, bass.ds(j, 1)], min_val=0, max_val=XS_ROWS - L)
                sp.dma_start(xb[:, b, :], xs[bass.ds(r, L), :]).then_inc(s_xb[b], 16)

            for j in range(NX):
                load_block(j, j)
            with sp.Fori(0, NBLK // NX - 1) as i:
                for b in range(NX):
                    sp.wait_ge(s_sc2[b], 16 * (i + 1))
                    load_block(i * NX + (b + NX), b)
            for j in range(NBLK // NX * NX, NBLK):
                sp.wait_ge(s_sc2[j % NX], 16 * (j // NX))
                load_block(j, j % NX)
            for b in range(NX):
                sp.wait_ge(s_sc2[b], 16 * len(range(b, NBLK, NX)))
            for q in range(NQ):
                for k in range(2):
                    sp.dma_start(yin[:, q, k, :, :], yv[:, k, q * Q:q * Q + Q, :]).then_inc(s_yin[q], 16)
            for q in range(NQ):
                sp.wait_ge(s_fin, q + 1)
                sp.dma_start(ov[:, q * Q:q * Q + Q, :], x_res[:, q * Q:q * Q + Q, :]).then_inc(s_out, 16)
            sp.wait_ge(s_out, 16 * NQ)

        @block.gpsimd
        def _(pool):
            pool.memset(halfn[:, :], -0.5).then_inc(s_setup, 1)
            pool.memset(one16[:, :], 1.0).then_inc(s_setup, 1)
            pool.memset(ones[:, :], 1.0).then_inc(s_setup, 1)
            pool.memset(P1[:, :, :, S:128], 0.0).then_inc(s_setup, 1)
            pool.memset(acc[:, 0, :], 0.0).then_inc(s_setup, 1)
            pool.memset(sr[:, :, :], 0.0).then_inc(s_setup, 1)
            pool.memset(mx[:, :, :], 0.0).then_inc(s_setup, 1)
            pool.memset(rs[:, :, :], 1.0).then_inc(s_setup, 1)
            pool.wait_ge(s_setup, 8)

            def power(n, g, have, done):
                pool.wait_ge(have, g + 1)
                pool.tensor_tensor(rstd[:, n, g % 2, :], var[:, n, g % 2, :], halfn[:, :],
                                   ALU.pow).then_inc(done, 1)

            power(0, 0, s_var1, s_rstd1)
            pool.memset(pad[:, :, :], 0.0).then_inc(s_padz, 1)
            pool.wait_ge(s_pad, 16)
            pool.wait_ge(s_padz, 1)
            pool.tensor_copy(pad[:, :, D:D + 1].rearrange("p i a -> p (i a)"), pad_i[:, :]).then_inc(s_padm, 1)
            for i in range(NG + 3):
                g = i - 3
                if g >= 0:
                    power(1, g, s_var2, s_rstd2)
                if i + 1 < NG:
                    power(0, i + 1, s_var1, s_rstd1)
                if g >= 0:
                    if g % 2:
                        q = g // 2
                        pool.wait_ge(s_pos, q + 1)
                        pool.wait_ge(s_rows, g + 1)
                        for j in range(Q):
                            for k in range(2):
                                pool.indirect_dma_start(
                                    xs, bass.IndirectOffsetOnAxis(ap=pos[:, q, k, j:j + 1], axis=0),
                                    rows[:, q * Q + j, k, :], None).then_inc(s_scat, 16)

            def scatter(j, b):
                pool.wait_ge(s_f10, j + 1)
                pool.sem_inc(s_seen, 1)
                pool.indirect_dma_start(
                    ys, bass.IndirectOffsetOnAxis(ap=xb[:, b, D:D + 1].bitcast(I32), axis=0),
                    yb[:, b, :], None).then_inc(s_sc2[b], 16)

            with pool.Fori(0, NBLK // NX) as i:
                for b in range(NX):
                    scatter(i * NX + b, b)
            for j in range(NBLK // NX * NX, NBLK):
                scatter(j, j % NX)

        @block.scalar
        def _(act):
            act.dma_start(cst[:, :], consts).then_inc(s_cst, 16)
            act.dma_start(b1_p[:, :], b1).then_inc(s_b1, 16)
            act.dma_start(dest[:, :, :], dests).then_inc(s_dest, 16)
            act.dma_start(pad_i[:, :], pads).then_inc(s_pad, 16)
            act.wait_ge(s_cst, 16)
            act.activation(lt16[:, :], cst[:, C_LT:C_LT + 128], ACT.Copy).then_inc(s_folded, 1)
            act.wait_ge(s_pack, 16)
            act.activation(tgx, V["g_x"], ACT.Tanh).then_inc(s_folded, 1)
            act.activation(tgf, V["g_f"], ACT.Tanh).then_inc(s_folded, 1)
            act.wait_ge(s_fold, 1)
            for i, dst in enumerate((A1T, A2T, U1)):
                act.activation(dst[:, :], bank[0][:, i * D:i * D + D], ACT.Copy).then_inc(s_folded, 1)
            act.wait_ge(s_fold, 2)
            for i, dst in enumerate((AG1T, AG2T)):
                act.activation(dst[:, :], bank[1][:, i * D:i * D + D], ACT.Copy).then_inc(s_folded, 1)
            act.wait_ge(s_fold, 3)
            for i, (dst, sc) in enumerate(((g1b, 1.0), (g2b, 1.0), (u2, 1.0), (k1s, SCALE), (k2s, SCALE), (bth, 0.5))):
                ins = act.activation(dst, bank[2][:, i:i + 1], ACT.Copy, scale=sc)
                ins.then_inc(s_folded, 1)
            act.wait_ge(s_folded, 14)
            act.wait_ge(s_setup, 8)
            for p in range(2):
                for j in range(G):
                    act.activation(sr[:, p, j:j + 1], k1s, ACT.Copy).then_inc(s_folded, 1)

            def A2(g):
                act.wait_ge(s_tp, g + 1)
                if g >= 2:
                    act.wait_ge(s_sc, g - 1)
                act.activation(tT[:, g % 2, :], bank[0][:, 0:G * L + G * S], ACT.Copy).then_inc(s_tT, 1)

            def A4(g):
                p = g % 2
                act.wait_ge(s_g, g + 1)
                if g >= 2:
                    act.wait_ge(s_sc, g - 1)
                    act.wait_ge(s_nb, g - 1)
                act.activation(Gs[:, p, 0, :], bank[1][:, 0:G * S], ACT.Identity, bias=g1b).then_inc(s_gs, 1)
                act.activation(Gs[:, p, 1, :], bank[1][:, G * S:2 * G * S], ACT.Identity, bias=g2b).then_inc(s_gs, 1)
                act.activation(sr[0:S, p, G:2 * G], bank[1][0:S, 2 * G * S:2 * G * S + G], ACT.Identity,
                               bias=k2s[0:S, :], scale=SCALE).then_inc(s_gs, 1)

            def B2(g):
                p = g % 2
                act.wait_ge(s_nb, g + 1)
                if g >= 2:
                    act.wait_ge(s_pt, g - 1)
                for j in range(G):
                    act.activation(P1[:, p, j, 0:S], bank[2][:, j * S:j * S + S], ACT.Exp, bias=nb[:, p, j:j + 1],
                                   scale=SCALE, accum_out=rs[:, p, j:j + 1])
                for j in range(G):
                    ins = act.activation(P2[:, p, j, :], bank[2][0:S, 256 + j * L:256 + j * L + L], ACT.Exp,
                                         bias=nb[0:S, p, G + j:G + j + 1], scale=SCALE,
                                         accum_out=rs[0:S, p, G + j:G + j + 1])
                ins.then_inc(s_exp, 1)

            def B5(g):
                act.wait_ge(s_pt, g + 1)
                if g >= 2:
                    act.wait_ge(s_t, g - 1)
                act.activation(PT[:, g % 2, :, :, :].rearrange("p a b c -> p (a b c)"), bank[3][:, :],
                               ACT.Copy).then_inc(s_ptc, 1)

            def C2(g):
                p = g % 2
                act.wait_ge(s_mixp, g + 1)
                if g >= 2:
                    act.wait_ge(s_mix, g - 1)
                act.activation(s2c[:, p, :], bank[5][:, 256:512], ACT.Identity, bias=V["bv_c"])
                act.activation(th[:, p, :], bank[6][:, 0:256], ACT.Tanh, bias=bth, scale=0.5).then_inc(s_gate, 1)

            def D5(g):
                act.wait_ge(s_x3p, g + 1)
                if g >= 2:
                    act.wait_ge(s_lg, g - 1)
                act.activation(x3T[:, g % 2, :], bank[7][:, 0:256], ACT.Copy).then_inc(s_x3T, 1)

            for i in range(NG + 3):
                if i < NG:
                    A2(i)
                if 0 <= i - 2 < NG:
                    C2(i - 2)
                if i < NG:
                    A4(i)
                if 0 <= i - 1 < NG:
                    B5(i - 1)
                if 0 <= i - 3 < NG:
                    D5(i - 3)
                if i < NG:
                    B2(i)
                if i < NG:
                    if i == 0:
                        act.wait_ge(s_w01[0], 16)
                    if i == E // 2:
                        act.wait_ge(s_w01[1], 16)
                    act.activation(w01_h[:, i, :], w01_f[:, i, :], ACT.Copy).then_inc(s_wsp, 1)
            act.wait_ge(s_wts, 1)
            act.activation(wd[:, 1, :], wd[:, 0, :], ACT.Exp).then_inc(s_wts, 1)

            act.preload_act_table(ACT.Silu)

            def F2(j, p):
                act.wait_ge(s_f1, j + 1)
                act.activation(xh[:, p, :], bank[0 + p][:, 0:128], ACT.Copy).then_inc(s_f2, 1)

            def F5(j, p):
                act.wait_ge(s_f4, j + 1)
                act.activation(sl[:, p, :], bank[2 + p][:, H:2 * H], ACT.Silu).then_inc(s_f5, 1)

            def F8(j, p):
                act.wait_ge(s_f7, j + 1)
                act.activation(aT[:, p, :], bank[4 + p][:, 0:H], ACT.Copy).then_inc(s_f8, 1)

            def slot(k, u):
                if not isinstance(k, int) or 1 <= k <= NBLK:
                    F8(k - 1, (u - 1) % 2)
                if not isinstance(k, int) or k + 3 < NBLK:
                    F2(k + 3, (u + 3) % 2)
                if not isinstance(k, int) or 0 <= k + 1 < NBLK:
                    F5(k + 1, (u + 1) % 2)

            for k in range(-3, FIRST):
                slot(k, k)
            with act.Fori(0, LOOPS) as i:
                for u in range(NX):
                    slot(i * NX + (u + FIRST), u + FIRST)
            for k in range(FIRST + LOOPS * NX, NBLK + 2):
                slot(k, k)

        @block.vector
        def _(dve):
            steps = [0]

            def link(ins):
                steps[0] += 1
                ins.then_inc(s_v, 1)
                dve.wait_ge(s_v, steps[0])

            def norm_stats(n, g, done):
                p = g % 2
                for j in range(G):
                    ins = dve.bn_stats(stat[:, n, p, j, :], x_res[:, G * g + j, :])
                link(ins)
                for j in range(G):
                    ins = dve.bn_aggr(mv[:, n, p, j, :], stat[:, n, p, j, :])
                link(ins)
                dve.tensor_scalar(var[:, n, p, :], mv[:, n, p, :, 1], EPS, None, ALU.add).then_inc(done, 1)

            def L1(g):
                dve.wait_ge(s_x0 if g == 0 else s_x[g // 2], 16)
                norm_stats(0, g, s_var1)

            def L2(g):
                p = g % 2
                dve.wait_ge(s_rstd1, g + 1)
                for j in range(G):
                    ins = dve.tensor_scalar(xln[:, G * g + j, :], x_res[:, G * g + j, :], mv[:, 0, p, j, 0:1],
                                            rstd[:, 0, p, j:j + 1], ALU.subtract, ALU.mult)
                ins.then_inc(s_xln, 1)

            def B1(g):
                p = g % 2
                dve.wait_ge(s_sc, g + 1)
                dve.wait_ge(s_gs, 3 * (g + 1))
                dve.tensor_reduce(mx[:, p, 0:G], bank[2][:, 0:G * S].rearrange("p (g s) -> p g s", g=G), AX, ALU.max)
                link(dve.tensor_reduce(mx[0:S, p, G:2 * G], bank[2][0:S, 256:512].rearrange("p (g s) -> p g s", g=G),
                                       AX, ALU.max))
                link(dve.scalar_tensor_tensor(tot[:, p, :], mx[:, p, :], SCALE, sr[:, p, :], ALU.mult, ALU.add))
                dve.tensor_tensor(nb[:, p, :], sr[:, p, :], tot[:, p, :], ALU.subtract).then_inc(s_nb, 1)

            def B3(g):
                p = g % 2
                dve.wait_ge(s_exp, g + 1)
                link(dve.reciprocal(rcp[:, p, :], rs[:, p, :]))
                for j in range(G):
                    dve.tensor_scalar(P1[:, p, j, 0:S], P1[:, p, j, 0:S], rcp[:, p, j:j + 1], None, ALU.mult)
                for j in range(G):
                    ins = dve.tensor_scalar(P2[:, p, j, :], P2[:, p, j, :], rcp[0:S, p, G + j:G + j + 1], None, ALU.mult)
                ins.then_inc(s_prob, 1)

            def B7(g):
                dve.wait_ge(s_t, g + 1)
                if g >= 2:
                    dve.wait_ge(s_mixp, g - 1)
                dve.tensor_copy(TT[:, g % 2, :, :].rearrange("p a b -> p (a b)"), bank[4][:, :]).then_inc(s_tt, 1)

            def C3(g):
                p = g % 2
                dve.wait_ge(s_gate, g + 1)
                if g >= 2:
                    dve.wait_ge(s_mT, g - 1)
                link(dve.scalar_tensor_tensor(dif[:, p, :], bank[5][:, 0:256], V["bv_s"], s2c[:, p, :],
                                              ALU.add, ALU.subtract))
                link(dve.scalar_tensor_tensor(gd[:, p, :], th[:, p, :], 1.0, dif[:, p, :], ALU.add, ALU.mult))
                dve.scalar_tensor_tensor(mix[:, p, :], gd[:, p, :], 0.5, s2c[:, p, :],
                                         ALU.mult, ALU.add).then_inc(s_mix, 1)

            def C5(g):
                dve.wait_ge(s_mT, g + 1)
                xg = x_res[:, G * g:G * g + G, :].rearrange("p b d -> p (b d)")
                dve.scalar_tensor_tensor(xg, bank[6][:, 256:512], tgx, xg, ALU.mult, ALU.add).then_inc(s_x2, 1)

            def D1(g):
                dve.wait_ge(s_x2, g + 1)
                norm_stats(1, g, s_var2)

            def D3(g):
                p = g % 2
                dve.wait_ge(s_rstd2, g + 1)
                for j in range(G):
                    ins = dve.tensor_scalar(rows[:, G * g + j, 0, 0:D], x_res[:, G * g + j, :], mv[:, 1, p, j, 0:1],
                                            rstd[:, 1, p, j:j + 1], ALU.subtract, ALU.mult)
                link(ins)
                dve.tensor_copy(rows[:, G * g:G * g + G, 1, 0:D], rows[:, G * g:G * g + G, 0, 0:D]).then_inc(s_rows, 1)

            def choose(k, src, m_out):
                link(dve.tensor_reduce(m_out, src, AX, ALU.max))
                link(dve.tensor_tensor(eq[:, :, :], src, m_out.rearrange("p (q a) -> p q a", a=1).to_broadcast([128, Q, E]), ALU.is_equal))
                rev = cst[:, C_REV:C_REV + E].rearrange("p (a e) -> p a e", a=1).to_broadcast([128, Q, E])
                link(dve.tensor_tensor(key[:, :, :], eq[:, :, :], rev, ALU.mult))
                link(dve.tensor_reduce(km[:, :], key[:, :, :], AX, ALU.max))
                link(dve.tensor_tensor(oh[:, k, :, :], key[:, :, :],
                                       km[:, :].rearrange("p (q a) -> p q a", a=1).to_broadcast([128, Q, E]), ALU.is_equal))

            def R1(q):
                dve.wait_ge(s_lg, 2 * q + 2)
                gb = gate_bB.rearrange("p (a e) -> p a e", a=1).to_broadcast([128, Q, E])
                ins = dve.tensor_tensor(lg[:, :, :], bank[7][:, 256:256 + Q * E].rearrange("p (q e) -> p q e", q=Q), gb, ALU.add)
                link(ins)
                choose(0, lg[:, :, :], m1[:, q * Q:q * Q + Q])
                link(dve.scalar_tensor_tensor(lg2[:, :, :], oh[:, 0, :, :], -FAR, lg[:, :, :], ALU.mult, ALU.add))
                choose(1, lg2[:, :, :], m2[:, q * Q:q * Q + Q])
                dve.tensor_tensor(ohs[:, :, :], oh[:, 0, :, :], oh[:, 1, :, :], ALU.add).then_inc(s_oh, 1)
                dve.wait_ge(s_oh, q + 1)
                link(dve.tensor_reduce(ohq[:, :], ohs[:, :, :].rearrange("p q e -> p e q"), AX, ALU.add))
                link(dve.tensor_tensor(acc[:, q + 1, :], acc[:, q, :], ohq[:, :], ALU.add))

            def R3(q):
                dve.wait_ge(s_rank, q + 1)
                base = cst[:, C_BASE:C_BASE + E].rearrange("p (a e) -> p a e", a=1).to_broadcast([128, Q, E])
                link(dve.tensor_tensor(rk[:, :, :], bank[7][:, 320:320 + Q * E].rearrange("p (q e) -> p q e", q=Q), base, ALU.add))
                for k in range(2):
                    ins = dve.tensor_tensor(prod[:, k, :, :], oh[:, k, :, :], rk[:, :, :], ALU.mult)
                link(ins)
                with nc.allow_low_precision(reason="whole numbers below 2**24, summed in float32"):
                    dve.tensor_reduce(pos[:, q, :, :], prod[:, :, :, :], AX, ALU.add).then_inc(s_pos, 1)

            dve.wait_ge(s_pack, 16)
            for i, n in enumerate(("bq_c", "bq_s")):
                ins = dve.tensor_copy(bq_rep[:, i, :], V[n].to_broadcast([128, D]))
            link(ins)
            L1(0)
            L2(0)
            dve.wait_ge(s_dest, 16)
            for k in range(2):
                dve.tensor_copy(rows[:, :, k, D:D + 1].bitcast(I32).rearrange("p b a -> p (b a)"), dest[:, k, :])
                dve.memset(rows[:, :, k, D + 1:ROW], 0.0)
            dve.wait_ge(s_folded, 18)
            dve.wait_ge(s_setup, 8)

            for i in range(NG + 3):
                if 0 <= i - 1 < NG:
                    B3(i - 1)
                if 0 <= i - 3 < NG:
                    D1(i - 3)
                if 0 <= i - 2 < NG:
                    C3(i - 2)
                if 0 <= i - 3 < NG:
                    D3(i - 3)
                if 0 <= i - 1 < NG:
                    B7(i - 1)
                if 0 <= i - 2 < NG:
                    C5(i - 2)
                if i + 1 < NG:
                    L1(i + 1)
                if i < NG:
                    B1(i)
                if i + 1 < NG:
                    L2(i + 1)
                if 0 <= i - 3 < NG and i % 2 == 0:
                    R1((i - 3) // 2)
                    R3((i - 3) // 2)
                if i < NG:
                    dve.wait_ge(s_wsp, i + 1)
                    dve.tensor_tensor(w01_l[:, i, :], w01_f[:, i, :], w01_h[:, i, :].bitcast(F32),
                                      ALU.subtract).then_inc(s_wsl, 1)
                if i == 0:
                    dve.wait_ge(s_b1, 16)
                    link(dve.tensor_copy(b1_3[:, 0, :], b1_p[:, :]))
                    link(dve.tensor_tensor(b1_r[:, 0, :], b1_p[:, :], b1_3[:, 0, :], ALU.subtract))
                    link(dve.tensor_copy(b1_3[:, 1, :], b1_r[:, 0, :]))
                    link(dve.tensor_tensor(b1_r[:, 1, :], b1_r[:, 0, :], b1_3[:, 1, :], ALU.subtract))
                    dve.tensor_copy(b1_3[:, 2, :], b1_r[:, 1, :]).then_inc(s_b1s, 1)

            link(dve.tensor_tensor(wd[:, 0, :], m2[:, :], m1[:, :], ALU.subtract))
            dve.sem_inc(s_wts, 1)

            dve.wait_ge(s_cnt, 1)
            dve.tensor_copy(nrow_i[:, :], bank[3][0:1, 8:8 + E]).then_inc(s_nrow, 1)
            link(dve.tensor_scalar(nbk_i[:, :], bank[3][0:E, 0:1], 1.0 / L, (L - 1.0) / L - 0.498, ALU.mult, ALU.add))
            dve.tensor_copy(nbk[:, :], nbk_i[:, :]).then_inc(s_tabv, 1)
            dve.wait_ge(s_tab, 1)
            link(dve.tensor_copy(bcum[:, :], bank[3][0:E, 1:2]))
            dve.tensor_scalar(cmp[:, :], cst[0:E, C_JS:C_JS + NBLK], bcum[:, 0:1], None, ALU.is_ge).then_inc(s_tabv, 1)
            dve.wait_ge(s_tab, 2)
            link(dve.tensor_copy(es[:, :, :].rearrange("p a j -> p (a j)"), bank[3][0:1, 16:16 + 2 * NBLK]))
            dve.tensor_scalar(e_i[:, :], es[:, 0, :], E - 1.0, None, ALU.min)
            dve.tensor_scalar(off[:, :], es[:, 0, :], float(LIST), None, ALU.mult).then_inc(s_tabv, 1)
            dve.wait_ge(s_tabv, 3)
            link(dve.scalar_tensor_tensor(off[:, :], es[:, 1, :], -float(L), off[:, :], ALU.mult, ALU.add))
            link(dve.scalar_tensor_tensor(r_i[:, :], cst[0:1, C_JS:C_JS + NBLK], float(L), off[:, :], ALU.mult, ALU.add))
            dve.sem_inc(s_table, 1)
            dve.wait_ge(s_b0, 16)
            dve.wait_ge(s_b2, 16)

            def F3(j, p):
                dve.wait_ge(s_f2, j + 1)
                dve.tensor_tensor(xl[:, p, :], bank[0 + p][:, 0:128], xh[:, p, :].bitcast(F32), ALU.subtract).then_inc(s_f3, 1)

            turn = [None]
            held = {}

            def expert(k, u):
                held[u] = dve.value_load(e_i[0:1, bass.ds(k, 1)], min_val=0, max_val=E - 1)

            def slot(k, u):
                loop = not isinstance(k, int)
                p, b = u % 2, (u - 2) % NX
                if loop or 0 <= k < NBLK:
                    b0e = b0_B[:, bass.ds(held[u], 1), :].rearrange("p a h -> p (a h)")
                    dve.wait_ge(s_f5, k + 1)
                    dve.tensor_tensor(hb[:, p, :], bank[2 + p][:, 0:H], b0e, ALU.add).then_inc(s_f6a, 1)
                if loop or k >= 2:
                    b2e = b2_B[:, bass.ds(held[u - 2], 1), :].rearrange("p a d -> p (a d)")
                    dve.wait_ge(s_f9, k - 1)
                    if loop or k - 2 >= NX:
                        dve.wait_ge(s_sc2[b], 16 * (turn[0] + (u - 2) // NX if loop else (k - 2) // NX))
                    dve.tensor_tensor(yb[:, b, :], bank[6 + p][:, 0:D], b2e, ALU.add).then_inc(s_f10, 1)
                if loop or 0 <= k < NBLK:
                    dve.wait_ge(s_f6a, k + 1)
                    dve.tensor_tensor(ab[:, p, :], hb[:, p, :], sl[:, p, :], ALU.mult).then_inc(s_f6, 1)
                if loop or 0 <= k + 1 < NBLK:
                    expert(k + 1, u + 1)
                if loop or 0 <= k + 2 < NBLK:
                    F3(k + 2, p)

            for k in range(-3, FIRST):
                slot(k, k)
            with dve.Fori(0, LOOPS) as i:
                turn[0] = i
                for u in range(FIRST - 2, FIRST + 1):
                    expert(i * NX + u, u)
                for u in range(FIRST, FIRST + NX):
                    slot(i * NX + u, u)
            last = FIRST + LOOPS * NX
            for k in range(last - 2, last + 1):
                expert(k, k)
            for k in range(last, NBLK + 2):
                slot(k, k)

            dve.wait_ge(s_wts, 2)
            link(dve.tensor_scalar(wd[:, 2, :], wd[:, 1, :], 1.0, None, ALU.add))
            link(dve.reciprocal(wd[:, 3, :], wd[:, 2, :]))
            link(dve.tensor_scalar(wd[:, 0, :], wd[:, 3, :], tgf, None, ALU.mult))
            link(dve.tensor_tensor(wd[:, 1, :], wd[:, 1, :], wd[:, 0, :], ALU.mult))

            for q in range(NQ):
                dve.wait_ge(s_yin[q], 32)
                for j in range(Q):
                    t = q * Q + j
                    ins = dve.scalar_tensor_tensor(o1[:, q, j, :], yin[:, q, 0, j, :], wd[:, 0, t:t + 1],
                                                   x_res[:, t, :], ALU.mult, ALU.add)
                link(ins)
                for j in range(Q):
                    t = q * Q + j
                    ins = dve.scalar_tensor_tensor(x_res[:, t, :], yin[:, q, 1, j, :], wd[:, 1, t:t + 1],
                                                   o1[:, q, j, :], ALU.mult, ALU.add)
                ins.then_inc(s_fin, 1)

        @block.tensor
        def _(pe):
            pe.wait_ge(s_pack, 16)
            pe.wait_ge(s_v, 1)
            bqr_c, bqr_s = bq_rep[:, 0, :], bq_rep[:, 1, :]
            pe.matmul(bank[0][:, 0:D], W["Wk_s"], W["Wq_c"], start=True, stop=True)
            pe.matmul(bank[0][:, D:2 * D], W["Wq_s"], W["Wk_c"], start=True, stop=True)
            pe.matmul(bank[0][:, 2 * D:3 * D], W["Wk_s"], bqr_c, start=True, stop=True).then_inc(s_fold, 1)
            pe.matmul(bank[1][:, 0:D], W["Wv_s"], W["WgT_1"], start=True, stop=True)
            pe.matmul(bank[1][:, D:2 * D], W["Wv_c"], W["WgT_2"], start=True, stop=True).then_inc(s_fold, 1)
            for i, (a, b) in enumerate(((W["Wq_c"], V["bk_s"]), (W["Wk_c"], V["bq_s"]), (W["Wq_s"], V["bk_c"]),
                                        (bqr_c, V["bk_s"]), (bqr_s, V["bk_c"]))):
                pe.matmul(bank[2][:, i:i + 1], a, b, start=True, stop=True)
            pe.wait_ge(s_cst, 16)
            pe.matmul(bank[2][:, 5:6], W["WgT_1"], V["bv_s"], start=True, stop=False)
            pe.matmul(bank[2][:, 5:6], W["WgT_2"], V["bv_c"], start=False, stop=False)
            pe.matmul(bank[2][:, 5:6], ident, V["bg"], start=False, stop=True).then_inc(s_fold, 1)
            pe.wait_ge(s_folded, 14)

            def A1(g):
                p = g % 2
                pe.wait_ge(s_c[0 if g < 2 else 1], 16)
                if g >= 1:
                    pe.wait_ge(s_tT, g)
                pe.wait_ge(s_xln, g + 1)
                for j in range(G):
                    pe.transpose(bank[0][:, G * L + j * S:G * L + j * S + S], c_in[:, G * g + j, :], cst[0:S, C_ID:C_ID + S])
                for j in range(G):
                    ins = pe.transpose(bank[0][:, j * L:j * L + L], xln[:, G * g + j, :], ident)
                ins.then_inc(s_tp, 1)

            def A3(g):
                p = g % 2
                pe.wait_ge(s_tT, g + 1)
                if g >= 1:
                    pe.wait_ge(s_gs, 3 * g)
                cT = tT[:, p, G * L:G * L + G * S]
                pe.matmul(bank[1][:, 0:G * S], A1T[:, :], cT, start=True, stop=True)
                pe.matmul(bank[1][:, G * S:2 * G * S], A2T[:, :], cT, start=True, stop=True)
                for j in range(G):
                    ins = pe.matmul(bank[1][0:S, 2 * G * S + j:2 * G * S + j + 1], cT[:, j * S:j * S + S], u2,
                                    start=True, stop=True)
                ins.then_inc(s_g, 1)

            def A5(g):
                p = g % 2
                pe.wait_ge(s_gs, 3 * (g + 1))
                if g >= 1:
                    pe.wait_ge(s_exp, g)
                cT = tT[:, p, G * L:G * L + G * S]
                pe.matmul(bank[2][:, 0:G * S], U1[:, :], cT, start=True, stop=False, skip_group_check=True)
                for j in range(G):
                    pe.matmul(bank[2][:, j * S:j * S + S], tT[:, p, j * L:j * L + L], Gs[:, p, 0, j * S:j * S + S],
                              start=False, stop=(j == G - 1), skip_group_check=True)
                for j in range(G):
                    ins = pe.matmul(bank[2][0:S, 256 + j * L:256 + j * L + L], Gs[:, p, 1, j * S:j * S + S],
                                    tT[:, p, j * L:j * L + L], start=True, stop=True)
                ins.then_inc(s_sc, 1)

            def B4(g):
                p = g % 2
                pe.wait_ge(s_prob, g + 1)
                if g >= 1:
                    pe.wait_ge(s_ptc, g)
                for j in range(G):
                    pe.transpose(bank[3][:, j * L:j * L + L], P1[:, p, j, :], ident)
                for j in range(G):
                    ins = pe.matmul(bank[3][:, 256 + j * L:256 + j * L + L], P2[:, p, j, :], interpT, start=True, stop=True)
                ins.then_inc(s_pt, 1)

            def B6(g):
                p = g % 2
                pe.wait_ge(s_ptc, g + 1)
                if g >= 1:
                    pe.wait_ge(s_tt, g)
                for j in range(G):
                    pe.matmul(bank[4][:, j * L:j * L + L], c_in[:, G * g + j, :], PT[0:S, p, 0, j, :], start=True, stop=True)
                for j in range(G):
                    ins = pe.matmul(bank[4][:, 256 + j * L:256 + j * L + L], xln[:, G * g + j, :], PT[:, p, 1, j, :],
                                    start=True, stop=True)
                ins.then_inc(s_t, 1)

            def C1(g):
                p = g % 2
                pe.wait_ge(s_tt, g + 1)
                if g >= 1:
                    pe.wait_ge(s_mix, g)
                    pe.wait_ge(s_x2, g)
                t1, t2 = TT[:, p, 0, :], TT[:, p, 1, :]
                pe.matmul(bank[5][:, 0:256], W["WvT_s"], t1, start=True, stop=True)
                pe.matmul(bank[5][:, 256:512], W["WvT_c"], t2, start=True, stop=True)
                pe.matmul(bank[6][:, 0:256], AG1T[:, :], t1, start=True, stop=False)
                pe.matmul(bank[6][:, 0:256], AG2T[:, :], t2, start=False, stop=True).then_inc(s_mixp, 1)

            def C4(g):
                p = g % 2
                pe.wait_ge(s_mix, g + 1)
                for j in range(G):
                    ins = pe.transpose(bank[6][:, 256 + j * L:256 + j * L + L], mix[:, p, j * L:j * L + L], ident)
                ins.then_inc(s_mT, 1)

            def D4(g):
                pe.wait_ge(s_rows, g + 1)
                if g >= 1:
                    pe.wait_ge(s_x3T, g)
                    if g % 2 == 0:
                        pe.wait_ge(s_pos, g // 2)
                for j in range(G):
                    ins = pe.transpose(bank[7][:, j * L:j * L + L], rows[:, G * g + j, 0, 0:D], ident)
                ins.then_inc(s_x3p, 1)

            def D6(g):
                p = g % 2
                pe.wait_ge(s_x3T, g + 1)
                for j in range(G):
                    o = 256 + (G * p + j) * E
                    ins = pe.matmul(bank[7][:, o:o + E], x3T[:, p, j * L:j * L + L], gate_wT, start=True, stop=True)
                ins.then_inc(s_lg, 1)

            def R2(q):
                pe.wait_ge(s_oh, q + 1)
                R = bank[7][:, 320:320 + Q * E].rearrange("p (q e) -> p q e", q=Q)
                pe.matmul(R, one16[:, :], acc[:, q, :].rearrange("p (a e) -> p a e", a=1).to_broadcast([128, Q, E]),
                          start=True, stop=False, skip_group_check=True)
                for j in range(Q - 1):
                    pe.matmul(R[:, j + 1:Q, :], one16[:, :],
                              ohs[:, j, :].rearrange("p (a e) -> p a e", a=1).to_broadcast([128, Q - 1 - j, E]),
                              start=False, stop=False, skip_group_check=True)
                pe.matmul(R, lt16[:, :], ohs[:, :, :], start=False, stop=True, skip_group_check=True).then_inc(s_rank, 1)

            for i in range(NG + 3):
                if i < NG:
                    A1(i)
                if 0 <= i - 2 < NG:
                    C1(i - 2)
                if 0 <= i - 1 < NG:
                    B4(i - 1)
                if i < NG:
                    A3(i)
                if 0 <= i - 3 < NG:
                    D4(i - 3)
                if 0 <= i - 1 < NG:
                    B6(i - 1)
                if i < NG:
                    A5(i)
                if 0 <= i - 2 < NG:
                    C4(i - 2)
                if 0 <= i - 3 < NG:
                    D6(i - 3)
                if 0 <= i - 3 < NG and i % 2 == 0:
                    R2((i - 3) // 2)

            pe.wait_ge(s_pos, NQ)
            pe.matmul(bank[3][0:E, 0:1], acc[:, NQ, :], one16[:, 0:1], start=True, stop=True)
            pe.matmul(bank[3][0:1, 8:8 + E], one16[:, 0:1], acc[:, NQ, :], start=True, stop=True).then_inc(s_cnt, 1)
            pe.wait_ge(s_tabv, 1)
            pe.wait_ge(s_nrow, 1)
            pe.matmul(bank[3][0:E, 1:2], cst[0:E, C_UT:C_UT + E], nbk[:, :], start=True, stop=True).then_inc(s_tab, 1)
            pe.wait_ge(s_tabv, 2)
            pe.matmul(bank[3][0:1, 16:16 + NBLK], ones[0:E, 0:1], cmp[:, :], start=True, stop=True)
            pe.matmul(bank[3][0:1, 16 + NBLK:16 + 2 * NBLK], nbk[:, :], cmp[:, :], start=True, stop=True).then_inc(s_tab, 1)

            pe.wait_ge(s_wsl, E)
            pe.wait_ge(s_w2, 16)
            pe.wait_ge(s_b1r, 48)
            pe.wait_ge(s_table, 1)

            def F1(j, p, b, n):
                pe.wait_ge(s_xb[b], n)
                pe.transpose(bank[0 + p][:, 0:128], xb[:, b, 0:D], ident).then_inc(s_f1, 1)

            def F4(j, p, e):
                pe.wait_ge(s_f3, j + 1)
                wh = w01_h[:, bass.ds(e, 1), :].rearrange("p a n -> p (a n)")
                wl = w01_l[:, bass.ds(e, 1), :].rearrange("p a n -> p (a n)")
                pe.matmul(bank[2 + p][:, :], xh[:, p, :], wh, start=True, stop=False, skip_group_check=True)
                pe.matmul(bank[2 + p][:, :], xh[:, p, :], wl, start=False, stop=False, skip_group_check=True)
                pe.matmul(bank[2 + p][:, :], xl[:, p, :], wh, start=False, stop=False, skip_group_check=True)
                b1e = b1_s[0:3, bass.ds(e, 1), :].rearrange("p a n -> p (a n)")
                pe.matmul(bank[2 + p][:, H:2 * H], one16[0:3, :], b1e, start=False, stop=True,
                          skip_group_check=True).then_inc(s_f4, 1)

            def F7(j, p):
                pe.wait_ge(s_f6, j + 1)
                for h in range(2):
                    ins = pe.transpose(bank[4 + p][:, h * 128:h * 128 + 128], ab[:, p, h * 128:h * 128 + 128], ident)
                ins.then_inc(s_f7, 1)

            def F9(j, p, e):
                pe.wait_ge(s_f8, j + 1)
                for h in range(2):
                    ins = pe.matmul(bank[6 + p][:, 0:D], aT[:, p, h * 128:h * 128 + 128],
                                    w2_f[:, bass.ds(e, 1), h, :].rearrange("p a n -> p (a n)"),
                                    start=(h == 0), stop=(h == 1))
                ins.then_inc(s_f9, 1)

            held = {}

            def expert(k, u):
                held[u] = pe.value_load(e_i[0:1, bass.ds(k, 1)], min_val=0, max_val=E - 1)

            def slot(k, u):
                if not isinstance(k, int) or 0 <= k + 1 < NBLK:
                    F4(k + 1, (u + 1) % 2, held[u + 1])
                if not isinstance(k, int) or 1 <= k <= NBLK:
                    F9(k - 1, (u - 1) % 2, held[u - 1])
                if not isinstance(k, int) or k + 3 < NBLK:
                    n = 16 * ((k + 3) // NX + 1) if isinstance(k, int) else 16 * (turn[0] + ((u + 3) // NX + 1))
                    F1(k + 3, (u + 3) % 2, (u + 3) % NX, n)
                if not isinstance(k, int) or 0 <= k + 2 < NBLK:
                    expert(k + 2, u + 2)
                if not isinstance(k, int) or 0 <= k < NBLK:
                    F7(k, u % 2)

            turn = [None]
            for k in range(-3, FIRST):
                slot(k, k)
            with pe.Fori(0, LOOPS) as i:
                turn[0] = i
                for u in range(FIRST - 1, FIRST + 2):
                    expert(i * NX + u, u)
                for u in range(FIRST, FIRST + NX):
                    slot(i * NX + u, u)
            last = FIRST + LOOPS * NX
            for k in range(last - 1, last + 2):
                expert(k, k)
            for k in range(last, NBLK + 2):
                slot(k, k)


def kernel(**inputs):
    import numpy as np
    import concourse.bacc as bacc
    from concourse.bass_utils import run_bass_kernel_spmd

    a = {k: np.asarray(v) for k, v in inputs.items()}
    f = np.float32

    def xa(n):
        return a["L0_xattn_" + n]

    def col(v):
        return np.broadcast_to(v.reshape(-1, 1), (128, 1))

    wgT = xa("Wg").T
    wpack = np.concatenate(
        [xa("Wq_c"), xa("Wk_s"), xa("Wq_s"), xa("Wk_c"), xa("Wv_s"), xa("Wv_c"), xa("Wv_s").T, xa("Wv_c").T,
         wgT[0:D], wgT[D:2 * D]]
        + [col(xa(n)) for n in ("bq_c", "bk_s", "bq_s", "bk_c", "bv_s", "bv_c", "bg")]
        + [col(a["g_xattn"]), col(a["g_ffn"]), a["L0_ffn_gate_w"].T,
           np.broadcast_to(a["L0_ffn_gate_b"].reshape(1, E), (128, E))], axis=1)
    w01 = np.concatenate([a["L0_ffn_w0"].transpose(2, 0, 1), a["L0_ffn_w1"].transpose(2, 0, 1)], axis=2)
    w2 = a["L0_ffn_w2"].reshape(E, D, 2, 128).transpose(3, 0, 2, 1)
    b1 = a["L0_ffn_b1"].reshape(128, E * H // 128)

    consts = np.zeros((128, N_CONST), f)
    consts[:, C_ID:C_ID + 128] = np.eye(128)
    at = np.clip((np.arange(L, dtype=f) + f(0.5)) * f(S / L) - f(0.5), f(0), f(S - 1))
    lo = np.floor(at).astype(np.int32)
    w = at - lo.astype(f)
    for i in range(L):
        consts[lo[i], C_IT + i] += f(1) - w[i]
        consts[min(lo[i] + 1, S - 1), C_IT + i] += w[i]
    consts[:, C_LT:C_LT + 128] = np.triu(np.ones((128, 128)), 1)
    consts[0:E, C_UT:C_UT + E] = np.triu(np.ones((E, E)))
    consts[:, C_REV:C_REV + E] = E - np.arange(E)
    consts[:, C_BASE:C_BASE + E] = np.arange(E) * LIST
    consts[:, C_JS:C_JS + NBLK] = np.arange(NBLK)
    tok = np.arange(B)[None, :] * L + np.arange(128)[:, None]
    dests = np.stack([tok, T + tok], axis=1).astype(np.int32)
    pads = (2 * T + np.arange(E + IDLE)[None, :] * L + np.arange(128)[:, None]).astype(np.int32).view(f)

    feeds = {"x": a["x"], "ctx_in": a["ctx_1024"], "wpack": wpack, "w01": w01, "w2": w2, "b0": a["L0_ffn_b0"],
             "b1": b1, "b2": a["L0_ffn_b2"], "consts": consts, "dests": dests, "pads": pads}
    nc = bacc.Bacc("TRN2", target_bir_lowering=False, num_devices=1)
    arrays, args = {}, []
    for name, v in feeds.items():
        v = np.ascontiguousarray(v)
        arrays[f"in_{name}"] = v
        args.append(nc.dram_tensor(f"in_{name}", v.shape, mybir.dt.from_np(v.dtype), kind="ExternalInput").ap())
    out = nc.dram_tensor("out", (B, L, D), F32, kind="ExternalOutput").ap()
    flamingo_kernel(nc, *args, out)
    r = run_bass_kernel_spmd(nc, [arrays], core_ids=[0])
    return r.results[0]["out"]
```

```python
from contextlib import ExitStack

import concourse.bass as bass
from concourse import mybir

F32 = mybir.dt.float32
F32R = mybir.dt.float32r
BF16 = mybir.dt.bfloat16
I32 = mybir.dt.int32
ALU = mybir.AluOpType
ACT = mybir.ActivationFunctionType
AX = mybir.AxisListType.X

B = 16
L = 128
D = 128
S = 77
E = 8
H = 256
G = 2
NG = B // G
NQ = NG // 2
T = B * L
CHUNKS = [(0, 2), (2, 4), (4, 8), (8, 12), (12, 14), (14, 16)]
SCALE = 1.0 / float(D) ** 0.5
EPS = 1e-5
OPENERS = 80
FAR = 1.0e30

LIST = T + L
NBLK = 2 * T // L + E - 1
NTAB = (NBLK + 3) // 4 * 4
NX = 8
IDLE = E - 1
ROW = D + 4
XS_ROWS = E * LIST + IDLE * L
Y_ROWS = 2 * T + (E + IDLE) * L

W_NAMES = ["Wq_c", "Wk_s", "Wq_s", "Wk_c", "Wv_s", "Wv_c", "WvT_s", "WvT_c", "WgT_1", "WgT_2"]
V_NAMES = ["bq_c", "bk_s", "bq_s", "bk_c", "bv_s", "bv_c", "bg", "g_x", "g_f"]
LAG = 8
N_PACK = len(W_NAMES) * D + len(V_NAMES) + 2 * E
FIRST_W = 4
N_FIRST = FIRST_W * D + len(V_NAMES) + 2 * E
C_ID, C_IT, C_LT, C_UT, C_REV, C_BASE, C_JS, C_LIST = 0, 128, 256, 384, 392, 400, 408, 408 + NBLK
N_CONST = C_LIST + E


def flamingo_kernel(nc, x, ctx_in, wpack, w01, w2, b0, b1, b2, consts, dests, pads, out):
    xs = nc.dram_tensor("xs_lists", (XS_ROWS, ROW), F32).ap()
    ys = nc.dram_tensor("y_rows", (Y_ROWS, D), F32).ap()
    stack = ExitStack()
    with stack:
        def sb(name, shape, dt=F32):
            return stack.enter_context(nc.sbuf_tensor(name, shape, dt))

        def sem(name):
            return stack.enter_context(nc.semaphore(name))

        x_res = sb("x_res", [128, B, D])
        c_in = sb("c_in", [S, B, D])
        pack = sb("pack", [128, N_PACK])
        cst = sb("cst", [128, N_CONST])
        dest = sb("dest", [128, 2, B], I32)
        pad = sb("pad", [128, E + IDLE, ROW])
        pad_i = sb("pad_i", [128, E + IDLE])
        W = {n: pack[:, o:o + D] for n, o in
             [(n, i * D) for i, n in enumerate(W_NAMES[:FIRST_W])]
             + [(n, N_FIRST + i * D) for i, n in enumerate(W_NAMES[FIRST_W:])]}
        V = {n: pack[:, FIRST_W * D + i:FIRST_W * D + i + 1] for i, n in enumerate(V_NAMES)}
        o = FIRST_W * D + len(V_NAMES)
        gate_wT, gate_bB = pack[:, o:o + E], pack[:, o + E:o + 2 * E]
        ident = cst[:, C_ID:C_ID + 128]
        interpT = cst[0:S, C_IT:C_IT + L]

        A1T = sb("A1T", [128, D])
        A2T = sb("A2T", [128, D])
        U1 = sb("U1", [128, D])
        AG1T = sb("AG1T", [128, D])
        AG2T = sb("AG2T", [128, D])
        bq_rep = sb("bq_rep", [128, 2, D])
        vec = sb("vec", [128, 8])
        g1b, g2b, u2, k1s, k2s, bth, tgx, tgf = (vec[:, i:i + 1] for i in range(8))
        lt16 = sb("lt16", [128, 128], BF16)
        one16 = sb("one16", [128, 128], BF16)
        ones = sb("ones", [128, 8])

        stat = sb("stat", [128, 2, B, 6])
        mv = sb("mv", [128, 2, B, 2])
        var = sb("var", [128, 2, B])
        rstd = sb("rstd", [128, 2, B])
        halfn = sb("halfn", [128, G])
        xln = sb("xln", [128, B, D])
        tT = sb("tT", [128, 2, G * L + G * S])
        Gs = sb("Gs", [128, 2, 2, G * S])
        sr = sb("sr", [128, NG, 2 * G])
        mx = sb("mx", [128, NG, 2 * G])
        tot = sb("tot", [128, NG, 2 * G])
        nb = sb("nb", [128, NG, 2 * G])
        rs = sb("rs", [128, NG, 2 * G])
        rcp = sb("rcp", [128, NG, 2 * G])
        P1 = sb("P1", [128, 2, G, 128])
        P2 = sb("P2", [S, 2, G, 128])
        PT = sb("PT", [128, 2, 2, G, 128])
        TT = sb("TT", [128, 2, 2, G * L])
        s2c = sb("s2c", [128, 2, G * L])
        th = sb("th", [128, 2, G * L])
        dif = sb("dif", [128, 2, G * L])
        gd = sb("gd", [128, 2, G * L])
        mix = sb("mix", [128, 2, G * L])
        rows = sb("rows", [128, B, 2, ROW])
        x3T = sb("x3T", [128, 2, G * L])

        Q = 2 * G
        lg = sb("lg", [128, G, E])
        lg2 = sb("lg2", [128, G, E])
        m1 = sb("m1", [128, B])
        m2 = sb("m2", [128, B])
        eq = sb("eq", [128, G, E])
        key = sb("key", [128, G, E])
        km = sb("km", [128, G])
        oh = sb("oh", [128, 2, G, E])
        hot = sb("hot", [128, NG + 1, G + 1, E], BF16)
        prod = sb("prod", [128, 2, G, E])
        pos = sb("pos", [128, NG, 2, G], I32)

        end_i = sb("end_i", [1, E], I32)
        nbk_i = sb("nbk_i", [E, 1], I32)
        nbk = sb("nbk", [E, 1])
        bcum = sb("bcum", [E, 1])
        cmp = sb("cmp", [E, NBLK])
        es = sb("es", [1, 2, NBLK])
        e_i = sb("e_i", [1, NTAB], I32)
        off = sb("off", [1, NBLK])
        r_i = sb("r_i", [1, NTAB], I32)
        wd = sb("wd", [128, 4, B])

        w01_f = sb("w01_f", [128, E, 2 * H])
        w01_h = sb("w01_h", [128, E, 2 * H], F32R)
        w01_l = sb("w01_l", [128, E, 2 * H], F32R)
        w2_f = sb("w2_f", [128, E, 2, D])
        b0_B = sb("b0_B", [128, E, H])
        b2_B = sb("b2_B", [128, E, D])
        b1_p = sb("b1_p", [128, E * H // 128])
        b1_r = sb("b1_r", [128, 2, E * H // 128])
        b1_3 = sb("b1_3", [128, 3, E * H // 128], BF16)
        b1_s = sb("b1_s", [3, E, H], BF16)
        
        xb = sb("xb", [128, NX, ROW])
        xh = sb("xh", [128, 2, 128], F32R)
        xl = sb("xl", [128, 2, 128], F32R)
        sl = sb("sl", [128, 2, H])
        hb = sb("hb", [128, 2, H])
        ab = sb("ab", [128, 2, H])
        aT = sb("aT", [128, 2, H])
        yb = sb("yb", [128, NX, D])
        yin = sb("yin", [128, 2, B, D])

        bank = [stack.enter_context(nc.psum_tensor(f"bank{i}", [128, 512], F32)) for i in range(8)]

        s_pack, s_cst, s_dest, s_pad, s_w2, s_b0, s_b1, s_b2 = (
            sem("in_" + n) for n in "pack cst dest pad w2 b0 b1 b2".split())
        s_w01 = [sem(f"in_w01_{h}") for h in range(2)]
        s_x = [sem(f"in_x{q}") for q in range(NQ)]
        s_c = [sem(f"in_c{h}") for h in range(2)]
        s_setup = sem("setup_memsets")
        s_fold = sem("fold_products")
        s_folded = sem("folded_weights")
        s_var1, s_rstd1, s_xln = sem("var1"), sem("rstd1"), sem("xln")
        s_tp, s_tT, s_g, s_gs, s_sc = sem("xc_transposed"), sem("xc_T_in_sbuf"), sem("G_made"), sem("G_in_sbuf"), sem("scores")
        s_nb, s_exp, s_prob = sem("neg_max"), sem("exps"), sem("probs")
        s_pt, s_ptc, s_t, s_tt = sem("probs_T"), sem("probs_T_in_sbuf"), sem("t_products"), sem("t_in_sbuf")
        s_mixp, s_gate, s_mix, s_mT, s_x2 = sem("mix_products"), sem("gate_tanh"), sem("mix"), sem("mix_T"), sem("x2")
        s_var2, s_rstd2, s_rows = sem("var2"), sem("rstd2"), sem("rows_ready")
        s_x3p, s_x3T, s_lg = sem("x3_transposed"), sem("x3T_in_sbuf"), sem("logits")
        s_cntg = sem("group_counts")
        s_copy = sem("rows_copied")
        s_lgr = sem("logits_read")
        s_bqr = sem("bq_spread")
        s_dst = sem("destinations_set")
        s_pack2 = sem("in_pack_rest")
        s_oh, s_rank, s_rkr, s_pos = sem("one_hots"), sem("ranks"), sem("ranks_read"), sem("positions")
        s_scat = sem("scattered")
        s_cnt, s_end, s_padw = sem("counts"), sem("list_ends"), sem("pads_written")
        s_tab = sem("table_products")
        s_tabv = sem("table_steps")
        s_table = sem("tables_ready")
        s_wsp = sem("w01_hi")
        s_wsl = sem("w01_lo")
        s_b1s = sem("b1_split")
        s_b1r = sem("b1_rows")
        s_x0 = sem("in_x_first_group")
        s_padm = sem("pads_made")
        s_padz = sem("pads_zero")
        s_xb = [sem(f"block_in{b}") for b in range(NX)]
        s_sc2 = [sem(f"block_out{b}") for b in range(NX)]
        s_f1, s_f2, s_f3, s_f4, s_f5, s_f6 = (sem(n) for n in "blk_xT blk_hi blk_lo blk_h blk_silu blk_act".split())
        s_f6a = sem("blk_h0")
        s_f7, s_f8, s_f9, s_f10 = (sem(n) for n in "blk_aT blk_aT_in_sbuf blk_y blk_y_in_sbuf".split())
        s_seen = sem("block_seen")
        s_yin = [[sem(f"y_in{k}_{c}") for c in range(len(CHUNKS))] for k in range(2)]
        s_y2 = sem("second_choice_weighted")
        s_o1 = sem("first_choice_added")
        s_fin = sem("final_rows")
        s_out = sem("stored")
        s_wts = sem("choice_weights")
        s_v = sem("vector_step")
        s_a = sem("scalar_step")

        def step(do, g):
            if 0 <= g < NG:
                do(g)

        lg_ps = bank[7][:, 256:256 + G * E].rearrange("p (q e) -> p q e", q=G)
        rk_ps = bank[0][:, 416:416 + G * E]

        def four(table, engine, most):
            return nc.values_load_multi_w_load_instructions(
                table, engines=[engine], min_val=0, max_val=most,
                skip_runtime_bounds_check_because="the table's entries are made within these bounds")[1]

        def write_pads(eng, engine, e0):
            for e, n in enumerate(four(end_i[0:1, e0:e0 + 4], engine, (E - 1) * LIST + T), start=e0):
                eng.dma_start(xs[bass.ds(n, L), :], pad[:, e, :]).then_inc(s_padw, 16)

        def stage(do, j):
            if 0 <= j < NBLK:
                do(j)

        block = stack.enter_context(nc.Block())

        xv = x.rearrange("b l d -> l b d")
        cv = ctx_in.rearrange("b l d -> l b d")
        ov = out.rearrange("b l d -> l b d")
        yv = ys[0:2 * T, :].rearrange("(k b l) d -> l k b d", k=2, b=B)

        @block.sync
        def _(sp):
            x0 = x_res[:, 0:Q, :]
            sp.dma_start(x0[:, 0:G, :], xv[:, 0:G, :]).then_inc(s_x0, 16)
            sp.dma_start(pack[:, 0:N_FIRST], wpack[:, 0:N_FIRST]).then_inc(s_pack, 16)
            sp.dma_start(c_in[:, 0:Q, :], cv[:, 0:Q, :]).then_inc(s_c[0], 16)
            sp.dma_start(x0[:, G:Q, :], xv[:, G:Q, :]).then_inc(s_x[0], 16)
            sp.dma_start(pack[:, N_FIRST:N_PACK], wpack[:, N_FIRST:N_PACK]).then_inc(s_pack2, 16)
            sp.dma_start(x_res[:, Q:2 * Q, :], xv[:, Q:2 * Q, :]).then_inc(s_x[1], 16)
            sp.dma_start(c_in[:, Q:B, :], cv[:, Q:B, :]).then_inc(s_c[1], 16)
            for q in range(2, NQ):
                sp.dma_start(x_res[:, q * Q:q * Q + Q, :], xv[:, q * Q:q * Q + Q, :]).then_inc(s_x[q], 16)
            sp.dma_start(w01_f[:, 0:E // 2, :], w01[:, 0:E // 2, :]).then_inc(s_w01[0], 16)
            sp.dma_start(w01_f[:, E // 2:E, :], w01[:, E // 2:E, :]).then_inc(s_w01[1], 16)
            sp.dma_start(w2_f[:, :, :, :], w2).then_inc(s_w2, 16)
            sp.dma_start(b0_B[:, :, :], b0.partition_broadcast(128)).then_inc(s_b0, 16)
            sp.dma_start(b2_B[:, :, :], b2.partition_broadcast(128)).then_inc(s_b2, 16)
            sp.wait_ge(s_b1s, 1)
            for n in range(3):
                sp.dma_start(b1_s[n:n + 1, :, :], b1_3[:, n, :]).then_inc(s_b1r, 16)
            sp.wait_ge(s_padm, 1)
            sp.dma_start(xs[E * LIST:XS_ROWS, :].rearrange("(i p) d -> p i d", p=L),
                         pad[:, E:E + IDLE, :]).then_inc(s_padw, 16)
            sp.wait_ge(s_end, 1)
            write_pads(sp, mybir.EngineType.SP, 0)
            sp.wait_ge(s_table, 1)
            first_row = four(r_i[0:1, 0:4], mybir.EngineType.SP, XS_ROWS - L)
            sp.wait_ge(s_padw, 16 * (E + 1))
            sp.wait_ge(s_scat, 16 * 2 * B)

            def load_block(j):
                sp.dma_start(xb[:, j % NX, :], xs[bass.ds(first_row[j % 4], L), :]).then_inc(s_xb[j % NX], 16)

            for j in range(NBLK):
                if j % 4 == 0 and j > 0:
                    first_row = four(r_i[0:1, j:j + 4], mybir.EngineType.SP, XS_ROWS - L)
                if j >= NX:
                    sp.wait_ge(s_sc2[j % NX], 16 * (j // NX))
                load_block(j)
            for b in range(NX):
                sp.wait_ge(s_sc2[b], 16 * len(range(b, NBLK, NX)))
            for c, (first, end) in enumerate(CHUNKS):
                for k in (1, 0):
                    sp.dma_start(yin[:, k, first:end, :], yv[:, k, first:end, :]).then_inc(s_yin[k][c], 16)
            for c, (first, end) in enumerate(CHUNKS):
                sp.wait_ge(s_fin, c + 1)
                sp.dma_start(ov[:, first:end, :], x_res[:, first:end, :]).then_inc(s_out, 16)
            sp.wait_ge(s_out, 16 * len(CHUNKS))

        @block.gpsimd
        def _(pool):
            pool.memset(halfn[:, :], -0.5).then_inc(s_setup, 1)
            pool.memset(one16[:, :], 1.0).then_inc(s_setup, 1)
            pool.memset(ones[:, :], 1.0).then_inc(s_setup, 1)
            pool.memset(P1[:, :, :, S:128], 0.0).then_inc(s_setup, 1)
            pool.memset(sr[:, :, :], 0.0).then_inc(s_setup, 1)
            pool.memset(mx[:, :, :], 0.0).then_inc(s_setup, 1)
            pool.memset(rs[:, :, :], 1.0).then_inc(s_setup, 1)
            pool.memset(e_i[:, :], 0).then_inc(s_setup, 1)
            pool.memset(r_i[:, :], 0).then_inc(s_setup, 1)
            pool.wait_ge(s_setup, 9)

            def power(n, g, have, done):
                pool.wait_ge(have, g + 1)
                pool.tensor_tensor(rstd[:, n, G * g:G * g + G], var[:, n, G * g:G * g + G], halfn[:, :],
                                   ALU.pow).then_inc(done, 1)

            def Lpw(g):
                power(0, g, s_var1, s_rstd1)

            def Dpw(g):
                power(1, g, s_var2, s_rstd2)

            def scatter_row(j, k):
                def scatter_batch(g):
                    if (j, k) == (0, 0):
                        if g == 0:
                            pool.wait_ge(s_dst, 1)
                        pool.wait_ge(s_pos, g + 1)
                        pool.wait_ge(s_copy, g + 1)
                    pool.indirect_dma_start(
                        xs, bass.IndirectOffsetOnAxis(ap=pos[:, g, k, j:j + 1], axis=0),
                        rows[:, G * g + j, k, :], None).then_inc(s_scat, 16)
                return scatter_batch

            pool.memset(pad[:, :, :], 0.0).then_inc(s_padz, 1)
            pool.wait_ge(s_pack, 16)
            for i, n in enumerate(("bq_c", "bq_s")):
                ins = pool.tensor_copy(bq_rep[:, i, :], V[n].to_broadcast([128, D]))
            ins.then_inc(s_bqr, 1)
            pool.wait_ge(s_pad, 16)
            pool.wait_ge(s_padz, 1)
            pool.tensor_copy(pad[:, :, D:D + 1].rearrange("p i a -> p (i a)"), pad_i[:, :]).then_inc(s_padm, 1)
            for i in range(NG + LAG):
                step(scatter_row(0, 0), i - 8)
                step(scatter_row(0, 1), i - 8)
                step(Lpw, i)
                step(Dpw, i - 6)
                step(scatter_row(1, 0), i - 8)
                step(scatter_row(1, 1), i - 8)
            def scatter(j, b):
                pool.wait_ge(s_f10, j + 1)
                pool.sem_inc(s_seen, 1)
                pool.indirect_dma_start(
                    ys, bass.IndirectOffsetOnAxis(ap=xb[:, b, D:D + 1].bitcast(I32), axis=0),
                    yb[:, b, :], None).then_inc(s_sc2[b], 16)

            for j in range(NBLK):
                scatter(j, j % NX)

        @block.scalar
        def _(act):
            act.dma_start(cst[:, :], consts).then_inc(s_cst, 16)
            act.dma_start(b1_p[:, :], b1).then_inc(s_b1, 16)
            act.dma_start(dest[:, :, :], dests).then_inc(s_dest, 16)
            act.dma_start(pad_i[:, :], pads).then_inc(s_pad, 16)
            act.wait_ge(s_cst, 16)
            act.activation(lt16[:, :], cst[:, C_LT:C_LT + 128], ACT.Copy).then_inc(s_folded, 1)
            act.wait_ge(s_pack, 16)
            act.activation(tgx, V["g_x"], ACT.Tanh).then_inc(s_folded, 1)
            act.activation(tgf, V["g_f"], ACT.Tanh).then_inc(s_folded, 1)
            act.wait_ge(s_fold, 1)
            for i, dst in enumerate((A1T, A2T, U1)):
                act.activation(dst[:, :], bank[4][:, i * D:i * D + D], ACT.Copy).then_inc(s_folded, 1)
            act.wait_ge(s_fold, 2)
            for i, (dst, sc) in enumerate(((g1b, 1.0), (g2b, 1.0), (u2, 1.0), (k1s, SCALE), (k2s, SCALE))):
                ins = act.activation(dst, bank[2][:, i:i + 1], ACT.Copy, scale=sc)
                ins.then_inc(s_folded, 1)
            act.wait_ge(s_folded, 11)
            act.wait_ge(s_setup, 9)
            act.activation(sr[:, :, 0:G], k1s.rearrange("p (a b) -> p a b", a=1).to_broadcast([128, NG, G]),
                           ACT.Copy).then_inc(s_folded, 1)

            def round_weights(e):
                act.wait_ge(s_w01[e // (E // 2)], 16)
                act.activation(w01_h[:, e, :], w01_f[:, e, :], ACT.Copy).then_inc(s_wsp, 1)

            def copy_gate():
                act.wait_ge(s_fold, 3)
                for i, dst in enumerate((AG1T, AG2T)):
                    act.activation(dst[:, :], bank[5][:, i * D:i * D + D], ACT.Copy).then_inc(s_folded, 1)
                act.activation(bth, bank[6][:, 0:1], ACT.Copy, scale=0.5).then_inc(s_folded, 1)

            def A2(g):
                act.wait_ge(s_tp, g + 1)
                if g >= 2:
                    act.wait_ge(s_sc, g - 1)
                act.activation(tT[:, g % 2, :], bank[0][:, 0:G * L + G * S], ACT.Copy).then_inc(s_tT, 1)

            def A4(g):
                p = g % 2
                act.wait_ge(s_g, g + 1)
                if g >= 2:
                    act.wait_ge(s_sc, g - 1)
                act.activation(Gs[:, p, 0, :], bank[1][:, 0:G * S], ACT.Identity, bias=g1b).then_inc(s_gs, 1)
                act.activation(Gs[:, p, 1, :], bank[1][:, G * S:2 * G * S], ACT.Identity, bias=g2b).then_inc(s_gs, 1)
                act.activation(sr[0:S, g, G:2 * G], bank[1][0:S, 2 * G * S:2 * G * S + G], ACT.Identity,
                               bias=k2s[0:S, :], scale=SCALE).then_inc(s_gs, 1)

            def B2(g):
                p = g % 2
                act.wait_ge(s_nb, g + 1)
                if g >= 2:
                    act.wait_ge(s_pt, g - 1)
                for j in range(G):
                    act.activation(P1[:, p, j, 0:S], bank[2][:, j * S:j * S + S], ACT.Exp, bias=nb[:, g, j:j + 1],
                                   scale=SCALE, accum_out=rs[:, g, j:j + 1])
                for j in range(G):
                    ins = act.activation(P2[:, p, j, :], bank[2][0:S, 256 + j * L:256 + j * L + L], ACT.Exp,
                                         bias=nb[0:S, g, G + j:G + j + 1], scale=SCALE,
                                         accum_out=rs[0:S, g, G + j:G + j + 1])
                ins.then_inc(s_exp, 1)

            def B5(g):
                act.wait_ge(s_pt, g + 1)
                if g >= 2:
                    act.wait_ge(s_t, g - 1)
                act.activation(PT[:, g % 2, :, :, :].rearrange("p a b c -> p (a b c)"), bank[3][:, :],
                               ACT.Copy).then_inc(s_ptc, 1)

            def B7(g):
                act.wait_ge(s_t, g + 1)
                if g >= 2:
                    act.wait_ge(s_mixp, g - 1)
                act.activation(TT[:, g % 2, :, :].rearrange("p a b -> p (a b)"), bank[4][:, :], ACT.Copy).then_inc(s_tt, 1)

            def C2(g):
                p = g % 2
                act.wait_ge(s_mixp, g + 1)
                if g >= 2:
                    act.wait_ge(s_mix, g - 1)
                if g == 0:
                    act.wait_ge(s_folded, 15)
                act.activation(s2c[:, p, :], bank[5][:, 256:512], ACT.Identity, bias=V["bv_c"])
                act.activation(th[:, p, :], bank[6][:, 0:256], ACT.Tanh, bias=bth, scale=0.5).then_inc(s_gate, 1)

            def Dcp(g):
                act.wait_ge(s_rows, g + 1)
                act.activation(rows[:, G * g:G * g + G, 1, 0:D], rows[:, G * g:G * g + G, 0, 0:D], ACT.Copy).then_inc(s_copy, 1)

            def D5(g):
                act.wait_ge(s_x3p, g + 1)
                if g >= 2:
                    act.wait_ge(s_lg, g - 1)
                act.activation(x3T[:, g % 2, :], bank[7][:, 0:256], ACT.Copy).then_inc(s_x3T, 1)

            for i in range(NG + LAG):
                if i == 3:
                    copy_gate()
                step(A4, i - 1)
                step(A2, i)
                step(C2, i - 4)
                step(B5, i - 3)
                step(D5, i - 5)
                step(Dcp, i - 5)
                step(B7, i - 3)
                step(B2, i - 1)
            for e in range(E):
                round_weights(e)
            act.wait_ge(s_wts, 1)
            act.activation(wd[:, 1, :], wd[:, 0, :], ACT.Exp).then_inc(s_wts, 1)

            act.wait_ge(s_end, 1)
            act.wait_ge(s_padm, 1)
            write_pads(act, mybir.EngineType.Activation, 4)
            act.preload_act_table(ACT.Silu)

            def F2(j):
                act.wait_ge(s_f1, j + 1)
                act.activation(xh[:, j % 2, :], bank[j % 2][:, 0:128], ACT.Copy).then_inc(s_f2, 1)

            def F5(j):
                act.wait_ge(s_f4, j + 1)
                act.activation(sl[:, j % 2, :], bank[2 + j % 2][:, H:2 * H], ACT.Silu).then_inc(s_f5, 1)

            def F8(j):
                act.wait_ge(s_f7, j + 1)
                act.activation(aT[:, j % 2, :], bank[4 + j % 2][:, 0:H], ACT.Copy).then_inc(s_f8, 1)

            for k in range(-3, NBLK + 1):
                stage(F8, k - 1)
                stage(F5, k + 1)
                stage(F2, k + 3)

            act.wait_ge(s_wts, 3)
            for c, (first, end) in enumerate(CHUNKS):
                act.wait_ge(s_yin[1][c], 16)
                for t in range(first, end):
                    ins = act.activation(yin[:, 1, t, :], yin[:, 1, t, :], ACT.Copy, scale=wd[:, 1, t:t + 1])
                ins.then_inc(s_y2, 1)

        @block.vector
        def _(dve):
            def link(ins):
                did("link", ins)
                after("link")

            at = {}

            def did(name, ins, signal=s_v):
                counted[signal] = counted.get(signal, 0) + 1
                ins.then_inc(signal, 1)
                at[name] = (signal, counted[signal])

            counted = {}

            def after(name):
                dve.wait_ge(*at[name])

            def batches(g):
                return range(G * g, G * g + G)

            def stats(n, g):
                for j in batches(g):
                    ins = dve.bn_stats(stat[:, n, j, :], x_res[:, j, :])
                did(("stats", n), ins)

            def aggregate(n, g):
                after(("stats", n))
                for j in batches(g):
                    ins = dve.bn_aggr(mv[:, n, j, :], stat[:, n, j, :])
                did(("mean_var", n, g), ins)

            def variance(n, g, done):
                after(("mean_var", n, g))
                dve.tensor_scalar(var[:, n, G * g:G * g + G], mv[:, n, G * g:G * g + G, 1], EPS, None,
                                  ALU.add).then_inc(done, 1)

            def Lst(g):
                dve.wait_ge(s_x0 if g == 0 else s_x[g // 2], 16)
                stats(0, g)

            def Lag(g):
                aggregate(0, g)

            def Lva(g):
                variance(0, g, s_var1)

            def Lap(g):
                dve.wait_ge(s_rstd1, g + 1)
                for j in batches(g):
                    ins = dve.tensor_scalar(xln[:, j, :], x_res[:, j, :], mv[:, 0, j, 0:1], rstd[:, 0, j:j + 1],
                                            ALU.subtract, ALU.mult)
                ins.then_inc(s_xln, 1)

            def B1a(g):
                dve.wait_ge(s_sc, g + 1)
                dve.tensor_reduce(mx[:, g, 0:G], bank[2][:, 0:G * S].rearrange("p (g s) -> p g s", g=G), AX, ALU.max)
                did("max", dve.tensor_reduce(mx[0:S, g, G:2 * G], bank[2][0:S, 256:512].rearrange("p (g s) -> p g s", g=G),
                                             AX, ALU.max))

            def B1b(g):
                after("max")
                if g == 0:
                    dve.wait_ge(s_folded, 12)
                dve.wait_ge(s_gs, 3 * (g + 1))
                did("row_max", dve.scalar_tensor_tensor(tot[:, g, :], mx[:, g, :], SCALE, sr[:, g, :], ALU.mult, ALU.add))

            def B1c(g):
                after("row_max")
                dve.tensor_tensor(nb[:, g, :], sr[:, g, :], tot[:, g, :], ALU.subtract).then_inc(s_nb, 1)

            def B3a(g):
                dve.wait_ge(s_exp, g + 1)
                did("inverse", dve.reciprocal(rcp[:, g, :], rs[:, g, :]))

            def B3b(g):
                p = g % 2
                after("inverse")
                for j in range(G):
                    dve.tensor_scalar(P1[:, p, j, 0:S], P1[:, p, j, 0:S], rcp[:, g, j:j + 1], None, ALU.mult)
                for j in range(G):
                    ins = dve.tensor_scalar(P2[:, p, j, :], P2[:, p, j, :], rcp[0:S, g, G + j:G + j + 1], None, ALU.mult)
                ins.then_inc(s_prob, 1)

            def C3a(g):
                p = g % 2
                dve.wait_ge(s_gate, g + 1)
                did("dif", dve.scalar_tensor_tensor(dif[:, p, :], bank[5][:, 0:256], V["bv_s"], s2c[:, p, :],
                                                    ALU.add, ALU.subtract))

            def C3b(g):
                p = g % 2
                after("dif")
                did("gd", dve.scalar_tensor_tensor(gd[:, p, :], th[:, p, :], 1.0, dif[:, p, :], ALU.add, ALU.mult))

            def C3c(g):
                p = g % 2
                after("gd")
                if g >= 2:
                    dve.wait_ge(s_mT, g - 1)
                dve.scalar_tensor_tensor(mix[:, p, :], gd[:, p, :], 0.5, s2c[:, p, :],
                                         ALU.mult, ALU.add).then_inc(s_mix, 1)

            def C5(g):
                dve.wait_ge(s_mT, g + 1)
                xg = x_res[:, G * g:G * g + G, :].rearrange("p b d -> p (b d)")
                did(("x2", g), dve.scalar_tensor_tensor(xg, bank[6][:, 256:512], tgx, xg, ALU.mult, ALU.add), s_x2)

            def Dst(g):
                after(("x2", g))
                stats(1, g)

            def Dag(g):
                aggregate(1, g)

            def Dva(g):
                variance(1, g, s_var2)

            def Dap(g):
                dve.wait_ge(s_rstd2, g + 1)
                for j in batches(g):
                    ins = dve.tensor_scalar(rows[:, j, 0, 0:D], x_res[:, j, :], mv[:, 1, j, 0:1],
                                            rstd[:, 1, j:j + 1], ALU.subtract, ALU.mult)
                ins.then_inc(s_rows, 1)

            def batch_spread(v):
                return v.rearrange("p (q a) -> p q a", a=1).to_broadcast([128, G, E])

            def expert_row(v):
                return v.rearrange("p (a e) -> p a e", a=1).to_broadcast([128, G, E])

            logits = (lg[:, :, :], lg2[:, :, :])

            def largest(k, g):
                return (m1, m2)[k][:, G * g:G * g + G]

            def R_logits(g):
                dve.wait_ge(s_lg, g + 1)
                did("logits", dve.tensor_tensor(lg[:, :, :], lg_ps, expert_row(gate_bB), ALU.add), s_lgr)

            def R_max(k):
                def largest_logit(g):
                    after("masked" if k else "logits")
                    did("largest", dve.tensor_reduce(largest(k, g), logits[k], AX, ALU.max))
                return largest_logit

            def R_equal(k):
                def which_are_largest(g):
                    after("largest")
                    did("equal", dve.tensor_tensor(eq[:, :, :], logits[k], batch_spread(largest(k, g)), ALU.is_equal))
                return which_are_largest

            def R_key(g):
                after("equal")
                did("key", dve.tensor_tensor(key[:, :, :], eq[:, :, :], expert_row(cst[:, C_REV:C_REV + E]), ALU.mult))

            def R_first(g):
                after("key")
                did("first", dve.tensor_reduce(km[:, :], key[:, :, :], AX, ALU.max))

            def R_onehot(k):
                def first_of_equals(g):
                    after("first")
                    did(("onehot", k), dve.tensor_tensor(oh[:, k, :, :], key[:, :, :], batch_spread(km[:, :]), ALU.is_equal))
                return first_of_equals

            def R_mask(g):
                after(("onehot", 0))
                did("masked", dve.scalar_tensor_tensor(lg2[:, :, :], oh[:, 0, :, :], -FAR, lg[:, :, :], ALU.mult, ALU.add))

            def R_both(g):
                after(("onehot", 1))
                did("both", dve.tensor_tensor(hot[:, g, 0:G, :], oh[:, 0, :, :], oh[:, 1, :, :], ALU.add), s_oh)

            def R_count(g):
                after("both")
                after("counts")
                with nc.allow_low_precision(reason="whole numbers below 256"):
                    did("counts", dve.tensor_reduce(hot[:, g + 1, G, :], hot[:, g, :, :].rearrange("p q e -> p e q"),
                                                    AX, ALU.add), s_cntg)

            def R_place(g):
                dve.wait_ge(s_rank, g + 1)
                ranks = rk_ps.rearrange("p (a x) -> p a x", a=1).to_broadcast([128, 2, G * E])
                did("place", dve.tensor_tensor(prod[:, :, :, :].rearrange("p k q e -> p k (q e)"),
                                               oh[:, :, :, :].rearrange("p k q e -> p k (q e)"), ranks, ALU.mult), s_rkr)

            def R_pos(g):
                after("place")
                with nc.allow_low_precision(reason="whole numbers below 2**24, summed in float32"):
                    dve.tensor_reduce(pos[:, g, :, :], prod[:, :, :, :], AX, ALU.add).then_inc(s_pos, 1)

            def weight_rest(e):
                dve.wait_ge(s_wsp, e + 1)
                dve.tensor_tensor(w01_l[:, e, :], w01_f[:, e, :], w01_h[:, e, :].bitcast(F32),
                                  ALU.subtract).then_inc(s_wsl, 1)

            dve.wait_ge(s_setup, 9)

            def set_destinations():
                dve.wait_ge(s_cst, 16)
                did("counts", dve.tensor_copy(hot[:, 0, G, :], cst[:, C_BASE:C_BASE + E]))
                dve.wait_ge(s_dest, 16)
                for k in range(2):
                    dve.tensor_copy(rows[:, :, k, D:D + 1].bitcast(I32).rearrange("p b a -> p (b a)"), dest[:, k, :])
                    ins = dve.memset(rows[:, :, k, D + 1:ROW], 0.0)
                ins.then_inc(s_dst, 1)

            def split_b1():
                dve.wait_ge(s_b1, 16)
                link(dve.tensor_copy(b1_3[:, 0, :], b1_p[:, :]))
                link(dve.tensor_tensor(b1_r[:, 0, :], b1_p[:, :], b1_3[:, 0, :], ALU.subtract))
                link(dve.tensor_copy(b1_3[:, 1, :], b1_r[:, 0, :]))
                link(dve.tensor_tensor(b1_r[:, 1, :], b1_r[:, 0, :], b1_3[:, 1, :], ALU.subtract))
                dve.tensor_copy(b1_3[:, 2, :], b1_r[:, 1, :]).then_inc(s_b1s, 1)

            for i in range(NG + LAG):
                if i == 3:
                    set_destinations()
                    split_b1()
                step(Lst, i)
                step(R_key, i - 8)
                step(Dag, i - 7)
                step(R_first, i - 8)
                step(Lag, i)
                step(Lap, i - 1)
                step(R_onehot(0), i - 8)
                step(Dva, i - 7)
                step(R_mask, i - 8)
                step(R_max(1), i - 8)
                step(B3a, i - 4)
                step(R_equal(1), i - 8)
                step(B3b, i - 4)
                step(R_key, i - 8)
                step(Dap, i - 7)
                step(R_first, i - 8)
                step(C3a, i - 6)
                step(R_onehot(1), i - 8)
                step(C3b, i - 6)
                step(R_both, i - 8)
                step(C3c, i - 6)
                step(R_count, i - 8)
                step(B1a, i - 3)
                step(Lva, i)
                step(R_place, i - 8)
                step(B1b, i - 3)
                step(R_pos, i - 8)
                step(C5, i - 6)
                step(R_logits, i - 7)
                step(B1c, i - 3)
                step(R_max(0), i - 7)
                step(Dst, i - 6)
                step(R_equal(0), i - 7)

            link(dve.tensor_tensor(wd[:, 0, :], m2[:, :], m1[:, :], ALU.subtract))
            dve.sem_inc(s_wts, 1)

            dve.wait_ge(s_cnt, 1)
            dve.tensor_copy(end_i[:, :], bank[3][0:1, 8:8 + E]).then_inc(s_end, 1)
            link(dve.tensor_scalar(nbk_i[:, :], bank[3][0:E, 0:1], 1.0 / L, (L - 1.0) / L - 0.498, ALU.mult, ALU.add))
            dve.tensor_scalar(nbk[:, :], nbk_i[:, :], cst[0:E, C_LIST:C_LIST + 1], None, ALU.subtract).then_inc(s_tabv, 1)
            dve.wait_ge(s_tab, 1)
            link(dve.tensor_copy(bcum[:, :], bank[3][0:E, 1:2]))
            dve.tensor_scalar(cmp[:, :], cst[0:E, C_JS:C_JS + NBLK], bcum[:, 0:1], None, ALU.is_ge).then_inc(s_tabv, 1)
            dve.wait_ge(s_tab, 2)
            link(dve.tensor_copy(es[:, :, :].rearrange("p a j -> p (a j)"), bank[3][0:1, 16:16 + 2 * NBLK]))
            dve.tensor_scalar(e_i[:, 0:NBLK], es[:, 0, :], E - 1.0, None, ALU.min)
            dve.tensor_scalar(off[:, :], es[:, 0, :], float(LIST), None, ALU.mult).then_inc(s_tabv, 1)
            dve.wait_ge(s_tabv, 3)
            link(dve.scalar_tensor_tensor(off[:, :], es[:, 1, :], -float(L), off[:, :], ALU.mult, ALU.add))
            link(dve.scalar_tensor_tensor(r_i[:, 0:NBLK], cst[0:1, C_JS:C_JS + NBLK], float(L), off[:, :], ALU.mult, ALU.add))
            dve.sem_inc(s_table, 1)
            for e in range(0, E):
                weight_rest(e)
            dve.wait_ge(s_wts, 2)
            link(dve.tensor_scalar(wd[:, 2, :], wd[:, 1, :], 1.0, None, ALU.add))
            link(dve.reciprocal(wd[:, 3, :], wd[:, 2, :]))
            link(dve.tensor_scalar(wd[:, 0, :], wd[:, 3, :], tgf, None, ALU.mult))
            dve.tensor_tensor(wd[:, 1, :], wd[:, 1, :], wd[:, 0, :], ALU.mult).then_inc(s_wts, 1)

            dve.wait_ge(s_b0, 16)
            dve.wait_ge(s_b2, 16)

            expert = [None] * NTAB

            def load_expert(j):
                if j % 4 == 0:
                    expert[j:j + 4] = four(e_i[0:1, j:j + 4], mybir.EngineType.DVE, E - 1)

            def F3(j):
                p = j % 2
                dve.wait_ge(s_f2, j + 1)
                dve.tensor_tensor(xl[:, p, :], bank[p][:, 0:128], xh[:, p, :].bitcast(F32), ALU.subtract).then_inc(s_f3, 1)

            def F6a(j):
                p = j % 2
                b0e = b0_B[:, bass.ds(expert[j], 1), :].rearrange("p a h -> p (a h)")
                dve.wait_ge(s_f5, j + 1)
                dve.tensor_tensor(hb[:, p, :], bank[2 + p][:, 0:H], b0e, ALU.add).then_inc(s_f6a, 1)

            def F6b(j):
                p = j % 2
                dve.wait_ge(s_f6a, j + 1)
                dve.tensor_tensor(ab[:, p, :], hb[:, p, :], sl[:, p, :], ALU.mult).then_inc(s_f6, 1)

            def F10(j):
                b2e = b2_B[:, bass.ds(expert[j], 1), :].rearrange("p a d -> p (a d)")
                dve.wait_ge(s_f9, j + 1)
                if j >= NX:
                    dve.wait_ge(s_sc2[j % NX], 16 * (j // NX))
                dve.tensor_tensor(yb[:, j % NX, :], bank[6 + j % 2][:, 0:D], b2e, ALU.add).then_inc(s_f10, 1)

            for k in range(-2, NBLK + 2):
                stage(F6a, k)
                stage(F10, k - 2)
                stage(F6b, k)
                stage(load_expert, k + 1)
                stage(F3, k + 2)

            def first_choice(c):
                dve.wait_ge(s_yin[0][c], 16)
                for t in range(*CHUNKS[c]):
                    ins = dve.scalar_tensor_tensor(x_res[:, t, :], yin[:, 0, t, :], wd[:, 0, t:t + 1], x_res[:, t, :],
                                                   ALU.mult, ALU.add)
                did(("first", c), ins)

            def second_choice(c):
                first, end = CHUNKS[c]
                after(("first", c))
                dve.wait_ge(s_y2, c + 1)
                dve.tensor_tensor(x_res[:, first:end, :], x_res[:, first:end, :], yin[:, 1, first:end, :],
                                  ALU.add).then_inc(s_fin, 1)

            for c in range(len(CHUNKS)):
                first_choice(c)
                if c >= 1:
                    second_choice(c - 1)
            second_choice(len(CHUNKS) - 1)

        @block.tensor
        def _(pe):
            pe.wait_ge(s_pack, 16)
            bqr_c, bqr_s = bq_rep[:, 0, :], bq_rep[:, 1, :]
            pe.matmul(bank[4][:, 0:D], W["Wk_s"], W["Wq_c"], start=True, stop=True)
            pe.matmul(bank[4][:, D:2 * D], W["Wq_s"], W["Wk_c"], start=True, stop=True)
            pe.wait_ge(s_bqr, 1)
            pe.matmul(bank[4][:, 2 * D:3 * D], W["Wk_s"], bqr_c, start=True, stop=True).then_inc(s_fold, 1)
            for i, (a, b) in enumerate(((W["Wq_c"], V["bk_s"]), (W["Wk_c"], V["bq_s"]), (W["Wq_s"], V["bk_c"]),
                                        (bqr_c, V["bk_s"]), (bqr_s, V["bk_c"]))):
                ins = pe.matmul(bank[2][:, i:i + 1], a, b, start=True, stop=True)
            ins.then_inc(s_fold, 1)

            def fold_gate():
                pe.wait_ge(s_pack2, 16)
                pe.matmul(bank[5][:, 0:D], W["Wv_s"], W["WgT_1"], start=True, stop=True)
                pe.matmul(bank[5][:, D:2 * D], W["Wv_c"], W["WgT_2"], start=True, stop=True)
                pe.matmul(bank[6][:, 0:1], W["WgT_1"], V["bv_s"], start=True, stop=False)
                pe.matmul(bank[6][:, 0:1], W["WgT_2"], V["bv_c"], start=False, stop=False)
                pe.matmul(bank[6][:, 0:1], ident, V["bg"], start=False, stop=True).then_inc(s_fold, 1)

            issued = {"transposes": 0, "ranks": 0}

            def A1(g):
                issued["transposes"] += 1
                if issued["ranks"]:
                    pe.wait_ge(s_rkr, issued["ranks"])
                if g == 0:
                    pe.wait_ge(s_cst, 16)
                pe.wait_ge(s_c[0 if g < 2 else 1], 16)
                if g >= 1:
                    pe.wait_ge(s_tT, g)
                pe.wait_ge(s_xln, g + 1)
                for j in range(G):
                    pe.transpose(bank[0][:, G * L + j * S:G * L + j * S + S], c_in[:, G * g + j, :], cst[0:S, C_ID:C_ID + S])
                for j in range(G):
                    ins = pe.transpose(bank[0][:, j * L:j * L + L], xln[:, G * g + j, :], ident)
                ins.then_inc(s_tp, 1)

            def A3(g):
                p = g % 2
                if g == 0:
                    pe.wait_ge(s_folded, 11)
                pe.wait_ge(s_tT, g + 1)
                if g >= 1:
                    pe.wait_ge(s_gs, 3 * g)
                cT = tT[:, p, G * L:G * L + G * S]
                pe.matmul(bank[1][:, 0:G * S], A1T[:, :], cT, start=True, stop=True)
                pe.matmul(bank[1][:, G * S:2 * G * S], A2T[:, :], cT, start=True, stop=True)
                for j in range(G):
                    ins = pe.matmul(bank[1][0:S, 2 * G * S + j:2 * G * S + j + 1], cT[:, j * S:j * S + S], u2,
                                    start=True, stop=True)
                ins.then_inc(s_g, 1)

            def A5(g):
                p = g % 2
                pe.wait_ge(s_gs, 3 * (g + 1))
                if g >= 1:
                    pe.wait_ge(s_exp, g)
                cT = tT[:, p, G * L:G * L + G * S]
                pe.matmul(bank[2][:, 0:G * S], U1[:, :], cT, start=True, stop=False, skip_group_check=True)
                for j in range(G):
                    pe.matmul(bank[2][:, j * S:j * S + S], tT[:, p, j * L:j * L + L], Gs[:, p, 0, j * S:j * S + S],
                              start=False, stop=(j == G - 1), skip_group_check=True)
                for j in range(G):
                    ins = pe.matmul(bank[2][0:S, 256 + j * L:256 + j * L + L], Gs[:, p, 1, j * S:j * S + S],
                                    tT[:, p, j * L:j * L + L], start=True, stop=True)
                ins.then_inc(s_sc, 1)

            def B4(g):
                p = g % 2
                pe.wait_ge(s_prob, g + 1)
                if g >= 1:
                    pe.wait_ge(s_ptc, g)
                for j in range(G):
                    pe.transpose(bank[3][:, j * L:j * L + L], P1[:, p, j, :], ident)
                for j in range(G):
                    ins = pe.matmul(bank[3][:, 256 + j * L:256 + j * L + L], P2[:, p, j, :], interpT, start=True, stop=True)
                ins.then_inc(s_pt, 1)

            def B6(g):
                p = g % 2
                pe.wait_ge(s_ptc, g + 1)
                if g >= 1:
                    pe.wait_ge(s_tt, g)
                for j in range(G):
                    pe.matmul(bank[4][:, j * L:j * L + L], c_in[:, G * g + j, :], PT[0:S, p, 0, j, :], start=True, stop=True)
                for j in range(G):
                    ins = pe.matmul(bank[4][:, 256 + j * L:256 + j * L + L], xln[:, G * g + j, :], PT[:, p, 1, j, :],
                                    start=True, stop=True)
                ins.then_inc(s_t, 1)

            def C1(g):
                p = g % 2
                if g == 0:
                    pe.wait_ge(s_folded, 15)
                pe.wait_ge(s_tt, g + 1)
                if g >= 1:
                    pe.wait_ge(s_mix, g)
                    pe.wait_ge(s_x2, g)
                t1, t2 = TT[:, p, 0, :], TT[:, p, 1, :]
                pe.matmul(bank[5][:, 0:256], W["WvT_s"], t1, start=True, stop=True)
                pe.matmul(bank[5][:, 256:512], W["WvT_c"], t2, start=True, stop=True)
                pe.matmul(bank[6][:, 0:256], AG1T[:, :], t1, start=True, stop=False)
                pe.matmul(bank[6][:, 0:256], AG2T[:, :], t2, start=False, stop=True).then_inc(s_mixp, 1)

            def C4(g):
                p = g % 2
                pe.wait_ge(s_mix, g + 1)
                for j in range(G):
                    ins = pe.transpose(bank[6][:, 256 + j * L:256 + j * L + L], mix[:, p, j * L:j * L + L], ident)
                ins.then_inc(s_mT, 1)

            def D4(g):
                pe.wait_ge(s_rows, g + 1)
                if g >= 1:
                    pe.wait_ge(s_x3T, g)
                    pe.wait_ge(s_lgr, g)
                for j in range(G):
                    ins = pe.transpose(bank[7][:, j * L:j * L + L], rows[:, G * g + j, 0, 0:D], ident)
                ins.then_inc(s_x3p, 1)

            def D6(g):
                p = g % 2
                pe.wait_ge(s_x3T, g + 1)
                for j in range(G):
                    ins = pe.matmul(lg_ps[:, j, :], x3T[:, p, j * L:j * L + L], gate_wT, start=True, stop=True)
                ins.then_inc(s_lg, 1)

            def R2(g):
                issued["ranks"] += 1
                pe.wait_ge(s_tT, issued["transposes"])
                pe.wait_ge(s_oh, g + 1)
                if g == 0:
                    pe.wait_ge(s_dst, 1)
                else:
                    pe.wait_ge(s_cntg, g)
                R = rk_ps.rearrange("p (q e) -> p q e", q=G)
                pe.matmul(R, one16[:, :], hot[:, g, G:G + 1, :].to_broadcast([128, G, E]),
                          start=True, stop=False, skip_group_check=True)
                for j in range(G - 1):
                    pe.matmul(R[:, j + 1:G, :], one16[:, :], hot[:, g, j:j + 1, :].to_broadcast([128, G - 1 - j, E]),
                              start=False, stop=False, skip_group_check=True)
                pe.matmul(R, lt16[:, :], hot[:, g, 0:G, :], start=False, stop=True, skip_group_check=True).then_inc(s_rank, 1)

            for i in range(NG + LAG):
                if i == 4:
                    fold_gate()
                step(R2, i - 8)
                step(C4, i - 6)
                step(D6, i - 7)
                step(A3, i - 2)
                step(A1, i - 1)
                step(C1, i - 5)
                step(B4, i - 4)
                step(A5, i - 2)
                step(D4, i - 6)
                step(B6, i - 4)

            pe.wait_ge(s_cntg, NG)
            pe.matmul(bank[3][0:E, 0:1], hot[:, NG, G, :], one16[:, 0:1], start=True, stop=True)
            pe.matmul(bank[3][0:1, 8:8 + E], one16[:, 0:1], hot[:, NG, G, :], start=True, stop=True).then_inc(s_cnt, 1)
            pe.wait_ge(s_tabv, 1)
            pe.wait_ge(s_end, 1)
            pe.matmul(bank[3][0:E, 1:2], cst[0:E, C_UT:C_UT + E], nbk[:, :], start=True, stop=True).then_inc(s_tab, 1)
            pe.wait_ge(s_tabv, 2)
            pe.matmul(bank[3][0:1, 16:16 + NBLK], ones[0:E, 0:1], cmp[:, :], start=True, stop=True)
            pe.matmul(bank[3][0:1, 16 + NBLK:16 + 2 * NBLK], nbk[:, :], cmp[:, :], start=True, stop=True).then_inc(s_tab, 1)

            for _ in range(OPENERS):
                pe.matmul(bank[0][:, 0:128], one16[:, :], one16[:, :], start=True, stop=True)


            expert = [None] * NTAB

            def load_expert(j):
                if j == 0:
                    pe.wait_ge(s_table, 1)
                if j % 4 == 0:
                    expert[j:j + 4] = four(e_i[0:1, j:j + 4], mybir.EngineType.PE, E - 1)

            def F1(j):
                pe.wait_ge(s_xb[j % NX], 16 * (j // NX + 1))
                pe.transpose(bank[j % 2][:, 0:128], xb[:, j % NX, 0:D], ident).then_inc(s_f1, 1)

            def F4(j):
                p, e = j % 2, bass.ds(expert[j], 1)
                if j == 0:
                    pe.wait_ge(s_wsl, E)
                    pe.wait_ge(s_b1r, 48)
                    pe.wait_ge(s_w2, 16)
                pe.wait_ge(s_f3, j + 1)
                wh = w01_h[:, e, :].rearrange("p a n -> p (a n)")
                wl = w01_l[:, e, :].rearrange("p a n -> p (a n)")
                pe.matmul(bank[2 + p][:, :], xh[:, p, :], wh, start=True, stop=False, skip_group_check=True)
                pe.matmul(bank[2 + p][:, :], xh[:, p, :], wl, start=False, stop=False, skip_group_check=True)
                pe.matmul(bank[2 + p][:, :], xl[:, p, :], wh, start=False, stop=False, skip_group_check=True)
                b1e = b1_s[0:3, e, :].rearrange("p a n -> p (a n)")
                pe.matmul(bank[2 + p][:, H:2 * H], one16[0:3, :], b1e, start=False, stop=True,
                          skip_group_check=True).then_inc(s_f4, 1)

            def F7(j):
                p = j % 2
                pe.wait_ge(s_f6, j + 1)
                for h in range(2):
                    ins = pe.transpose(bank[4 + p][:, h * 128:h * 128 + 128], ab[:, p, h * 128:h * 128 + 128], ident)
                ins.then_inc(s_f7, 1)

            def F9(j):
                p, e = j % 2, bass.ds(expert[j], 1)
                pe.wait_ge(s_f8, j + 1)
                for h in range(2):
                    ins = pe.matmul(bank[6 + p][:, 0:D], aT[:, p, h * 128:h * 128 + 128],
                                    w2_f[:, e, h, :].rearrange("p a n -> p (a n)"), start=(h == 0), stop=(h == 1))
                ins.then_inc(s_f9, 1)

            for k in range(-3, NBLK + 1):
                stage(F4, k + 1)
                stage(F9, k - 1)
                stage(F1, k + 3)
                stage(load_expert, k + 2)
                stage(F7, k)


def kernel(**inputs):
    import numpy as np
    import concourse.bacc as bacc
    from concourse.bass_utils import run_bass_kernel_spmd

    a = {k: np.asarray(v) for k, v in inputs.items()}
    f = np.float32

    def xa(n):
        return a["L0_xattn_" + n]

    def col(v):
        return np.broadcast_to(v.reshape(-1, 1), (128, 1))

    wgT = xa("Wg").T
    wpack = np.concatenate(
        [xa("Wq_c"), xa("Wk_s"), xa("Wq_s"), xa("Wk_c")]
        + [col(xa(n)) for n in ("bq_c", "bk_s", "bq_s", "bk_c", "bv_s", "bv_c", "bg")]
        + [col(a["g_xattn"]), col(a["g_ffn"]), a["L0_ffn_gate_w"].T,
           np.broadcast_to(a["L0_ffn_gate_b"].reshape(1, E), (128, E))]
        + [xa("Wv_s"), xa("Wv_c"), xa("Wv_s").T, xa("Wv_c").T, wgT[0:D], wgT[D:2 * D]], axis=1)
    w01 = np.concatenate([a["L0_ffn_w0"].transpose(2, 0, 1), a["L0_ffn_w1"].transpose(2, 0, 1)], axis=2)
    w2 = a["L0_ffn_w2"].reshape(E, D, 2, 128).transpose(3, 0, 2, 1)
    b1 = a["L0_ffn_b1"].reshape(128, E * H // 128)

    consts = np.zeros((128, N_CONST), f)
    consts[:, C_ID:C_ID + 128] = np.eye(128)
    at = np.clip((np.arange(L, dtype=f) + f(0.5)) * f(S / L) - f(0.5), f(0), f(S - 1))
    lo = np.floor(at).astype(np.int32)
    w = at - lo.astype(f)
    for i in range(L):
        consts[lo[i], C_IT + i] += f(1) - w[i]
        consts[min(lo[i] + 1, S - 1), C_IT + i] += w[i]
    consts[:, C_LT:C_LT + 128] = np.triu(np.ones((128, 128)), 1)
    consts[0:E, C_UT:C_UT + E] = np.triu(np.ones((E, E)))
    consts[:, C_REV:C_REV + E] = E - np.arange(E)
    consts[:, C_BASE:C_BASE + E] = np.arange(E) * (LIST // L)
    consts[0:E, C_LIST] = np.arange(E) * (LIST // L)
    consts[:, C_JS:C_JS + NBLK] = np.arange(NBLK)
    tok = np.arange(B)[None, :] * L + np.arange(128)[:, None]
    dests = np.stack([tok, T + tok], axis=1).astype(np.int32)
    pads = (2 * T + np.arange(E + IDLE)[None, :] * L + np.arange(128)[:, None]).astype(np.int32).view(f)

    feeds = {"x": a["x"], "ctx_in": a["ctx_1024"], "wpack": wpack, "w01": w01, "w2": w2, "b0": a["L0_ffn_b0"],
             "b1": b1, "b2": a["L0_ffn_b2"], "consts": consts, "dests": dests, "pads": pads}
    nc = bacc.Bacc("TRN2", target_bir_lowering=False, num_devices=1)
    arrays, args = {}, []
    for name, v in feeds.items():
        v = np.ascontiguousarray(v)
        arrays[f"in_{name}"] = v
        args.append(nc.dram_tensor(f"in_{name}", v.shape, mybir.dt.from_np(v.dtype), kind="ExternalInput").ap())
    out = nc.dram_tensor("out", (B, L, D), F32, kind="ExternalOutput").ap()
    flamingo_kernel(nc, *args, out)
    r = run_bass_kernel_spmd(nc, [arrays], core_ids=[0])
    return r.results[0]["out"]
```
